# Optimizing a Trainium2 kernel written in Bass

```python
import numpy as np
import jax
import jax.numpy as jnp

def _softmax(x, axis=-1):
    return jax.nn.softmax(x, axis=axis)

def _gelu(x):
    return jax.nn.gelu(x, approximate=True)

def _silu(x):
    return jax.nn.silu(x)

def _sigmoid(x):
    return jax.nn.sigmoid(x)

def _layernorm(x, axis=-1, eps=1e-05):
    m = jnp.mean(x, axis=axis, keepdims=True)
    v = jnp.var(x, axis=axis, keepdims=True)
    return (x - m) / jnp.sqrt(v + eps)

def _scatter_add(tgt, idx, src, axis=0):
    return tgt.at[idx].add(src)

def _segment_sum(src, seg, n):
    return jax.ops.segment_sum(src, seg, n)
kernel_name = 'mk_adj_resnorm_d4_adj_r2_15d699'

def setup_inputs(seed: int=0):
    np.random.seed(seed)
    _w = jnp.asarray

    def _rec_inputs():
        import jax
        import jax.numpy as jnp
        _gk = jax.random.key(seed)
        x = -0.000929 + 1 * jax.random.normal(jax.random.fold_in(_gk, 1), (4096, 128), jnp.float32)
        _w = (1.0 + jnp.arange(4096, dtype=jnp.float32)) ** (-0.5)
        _w = _w / _w.mean()
        _pij = jnp.clip(0.000976562 * _w[:, None] * _w[None, :], 0.0, 1.0)
        _a = jax.random.uniform(jax.random.fold_in(_gk, 2), (4096, 4096)) < _pij
        _a = jnp.logical_or(_a, jnp.eye(4096, dtype=bool))
        _af = _a.astype(jnp.float32)
        _af = _af * jax.random.uniform(jax.random.fold_in(_gk, 3), (4096, 4096), jnp.float32, 0.05, 1)
        adj = _af
        return (x, adj)
    x, adj = _rec_inputs()

    def _L0_gnn_setup():
        import jax, jax.numpy as jnp
        import numpy as np
        NEG_SLOPE = 0.01
        N_U, N_V = (4096, 4096)
        U_F, V_F = (128, 128)
        HIDS = [128, 128]
        NUM_ROUNDS = 3

        def _glorot(key, fan_in, fan_out):
            lim = np.sqrt(6.0 / (fan_in + fan_out)).astype(np.float32)
            return jax.random.uniform(key, (fan_in, fan_out), jnp.float32, -lim, lim)

        def _mlp(x, W1, b1, W2, b2, W3, b3):
            a = jax.nn.leaky_relu
            x = a(x @ W1 + b1, NEG_SLOPE)
            x = a(x @ W2 + b2, NEG_SLOPE)
            return a(x @ W3 + b3, NEG_SLOPE)
        key = jax.random.key(seed)
        ks = jax.random.split(key, 12)
        inp = {'u_node_feats': jax.random.normal(ks[0], (N_U, U_F), jnp.float32), 'v_node_feats': jax.random.normal(ks[1], (N_V, V_F), jnp.float32), 'uv_adj_mat': jax.random.uniform(ks[2], (N_V, N_U), jnp.float32), 'vu_adj_mat': jax.random.uniform(ks[3], (N_U, N_V), jnp.float32)}
        dims_uv = [U_F] + HIDS + [V_F]
        dims_vu = [V_F] + HIDS + [U_F]
        k = 4
        for tag, dims in (('uv', dims_uv), ('vu', dims_vu)):
            for i in range(3):
                inp[f'{tag}_W{i + 1}'] = _glorot(ks[k], dims[i], dims[i + 1])
                k += 1
                inp[f'{tag}_b{i + 1}'] = jnp.zeros((dims[i + 1],), jnp.float32)
        return inp
    _L0_gnn_all = _L0_gnn_setup()
    _L0_gnn_in = {k: v for k, v in _L0_gnn_all.items() if k in ('v_node_feats', 'uv_W1', 'uv_b1', 'uv_W2', 'uv_b2', 'uv_W3', 'uv_b3', 'vu_W1', 'vu_b1', 'vu_W2', 'vu_b2', 'vu_W3', 'vu_b3')}
    del _L0_gnn_all

    def _L1_gnn_setup():
        import jax, jax.numpy as jnp
        import numpy as np
        N, DIM = (8192, 128)

        def _gru_cell(x, h, W_ih, W_hh, b_ih, b_hh):
            gi = x @ W_ih.T + b_ih
            gh = h @ W_hh.T + b_hh
            i_r, i_z, i_n = jnp.split(gi, 3, axis=-1)
            h_r, h_z, h_n = jnp.split(gh, 3, axis=-1)
            r = jax.nn.sigmoid(i_r + h_r)
            z = jax.nn.sigmoid(i_z + h_z)
            n = jnp.tanh(i_n + r * h_n)
            return (1.0 - z) * n + z * h
        key = jax.random.key(seed)
        ks = jax.random.split(key, 8)
        states = jax.random.normal(ks[0], (N, DIM), dtype=jnp.float32)
        adj = jax.random.uniform(ks[1], (N, N), dtype=jnp.float32)
        s = 1.0 / np.sqrt(DIM)
        W_msg = jax.random.uniform(ks[2], (DIM, DIM), minval=-s, maxval=s, dtype=jnp.float32)
        b_msg = jax.random.uniform(ks[3], (DIM,), minval=-s, maxval=s, dtype=jnp.float32)
        W_ih = jax.random.uniform(ks[4], (3 * DIM, DIM), minval=-s, maxval=s, dtype=jnp.float32)
        W_hh = jax.random.uniform(ks[5], (3 * DIM, DIM), minval=-s, maxval=s, dtype=jnp.float32)
        b_ih = jax.random.uniform(ks[6], (3 * DIM,), minval=-s, maxval=s, dtype=jnp.float32)
        b_hh = jax.random.uniform(ks[7], (3 * DIM,), minval=-s, maxval=s, dtype=jnp.float32)
        return {'states': states, 'adj': adj, 'W_msg': W_msg, 'b_msg': b_msg, 'W_ih': W_ih, 'W_hh': W_hh, 'b_ih': b_ih, 'b_hh': b_hh}
    _L1_gnn_all = _L1_gnn_setup()
    _L1_gnn_in = {k: v for k, v in _L1_gnn_all.items() if k in ('W_msg', 'b_msg', 'W_ih', 'W_hh', 'b_ih', 'b_hh')}
    del _L1_gnn_all

    def _L2_gnn_setup():
        import jax, jax.numpy as jnp
        import numpy as np
        N = 8192
        IN_DIM = 128
        OUT_DIM = 128

        def _message(X, A, W):
            deg = jnp.sum(A, axis=1, keepdims=True)
            A_norm = A / jnp.where(deg > 0, deg, 1.0)
            return A_norm @ X @ W
        key = jax.random.key(seed)
        k1, k2, k3, k4 = jax.random.split(key, 4)
        X = jax.random.normal(k1, (N, IN_DIM), dtype=jnp.float32)
        A = jax.random.uniform(k2, (N, N), dtype=jnp.float32)
        W_in = jax.random.normal(k3, (IN_DIM, OUT_DIM), dtype=jnp.float32) / np.sqrt(IN_DIM)
        W_out = jax.random.normal(k4, (IN_DIM, OUT_DIM), dtype=jnp.float32) / np.sqrt(IN_DIM)
        return {'X': X, 'A': A, 'W_in': W_in, 'W_out': W_out}
    _L2_gnn_all = _L2_gnn_setup()
    _L2_gnn_in = {k: v for k, v in _L2_gnn_all.items() if k in ('W_in', 'W_out')}
    del _L2_gnn_all

    def _L3_gnn_setup():
        import jax, jax.numpy as jnp
        import numpy as np
        N, IN, H, C = (2048, 128, 4, 32)
        HC = H * C
        EDGE_P = 0.008

        def _linear_params(key, fan_in, fan_out, bias=True):
            k1, k2 = jax.random.split(key)
            lim = 1.0 / np.sqrt(fan_in)
            W = jax.random.uniform(k1, (fan_in, fan_out), jnp.float32, -lim, lim)
            if not bias:
                return W
            b = jax.random.uniform(k2, (fan_out,), jnp.float32, -lim, lim)
            return (W, b)

        def _transformer_conv(x, adj, Wq, bq, Wk, bk, Wv, bv, Ws, bs, Wb):
            n = x.shape[0]
            q = (x @ Wq + bq).reshape(n, H, C)
            k = (x @ Wk + bk).reshape(n, H, C)
            v = (x @ Wv + bv).reshape(n, H, C)
            attn = jnp.einsum('nhc,mhc->hnm', q, k) / np.float32(np.sqrt(C))
            mask = adj == 0.0
            neg = jnp.where(mask[None], -jnp.inf, attn)
            m = jnp.max(neg, axis=-1, keepdims=True)
            all_inf = jnp.isneginf(m)
            e = jnp.where(mask[None], 0.0, jnp.exp(neg - jnp.where(all_inf, 0.0, m)))
            denom = jnp.sum(e, axis=-1, keepdims=True)
            alpha = e / jnp.where(denom == 0.0, 1.0, denom)
            out = jnp.einsum('hnm,mhc->hnc', alpha, v)
            out = jnp.transpose(out, (1, 2, 0)).reshape(n, C * H)
            x_r = x @ Ws + bs
            beta = jax.nn.sigmoid(jnp.concatenate([out, x_r, out - x_r], axis=-1) @ Wb)
            return beta * x_r + (1.0 - beta) * out
        key = jax.random.key(seed)
        ks = jax.random.split(key, 7)
        x = jax.random.normal(ks[0], (N, IN), jnp.float32)
        adj = (jax.random.uniform(ks[1], (N, N)) < EDGE_P).astype(jnp.float32)
        Wq, bq = _linear_params(ks[2], IN, HC)
        Wk, bk = _linear_params(ks[3], IN, HC)
        Wv, bv = _linear_params(ks[4], IN, HC)
        Ws, bs = _linear_params(ks[5], IN, HC)
        Wb = _linear_params(ks[6], 3 * HC, 1, bias=False)
        return dict(x=x, adj=adj, Wq=Wq, bq=bq, Wk=Wk, bk=bk, Wv=Wv, bv=bv, Ws=Ws, bs=bs, Wb=Wb)
    _L3_gnn_all = _L3_gnn_setup()
    _L3_gnn_in = {k: v for k, v in _L3_gnn_all.items() if k in ('Wq', 'bq', 'Wk', 'bk', 'Wv', 'bv', 'Ws', 'bs', 'Wb')}
    del _L3_gnn_all
    return {'x': x, 'adj': adj, 'L0_gnn_v_node_feats': _L0_gnn_in['v_node_feats'], 'L0_gnn_uv_W1': _L0_gnn_in['uv_W1'], 'L0_gnn_uv_b1': _L0_gnn_in['uv_b1'], 'L0_gnn_uv_W2': _L0_gnn_in['uv_W2'], 'L0_gnn_uv_b2': _L0_gnn_in['uv_b2'], 'L0_gnn_uv_W3': _L0_gnn_in['uv_W3'], 'L0_gnn_uv_b3': _L0_gnn_in['uv_b3'], 'L0_gnn_vu_W1': _L0_gnn_in['vu_W1'], 'L0_gnn_vu_b1': _L0_gnn_in['vu_b1'], 'L0_gnn_vu_W2': _L0_gnn_in['vu_W2'], 'L0_gnn_vu_b2': _L0_gnn_in['vu_b2'], 'L0_gnn_vu_W3': _L0_gnn_in['vu_W3'], 'L0_gnn_vu_b3': _L0_gnn_in['vu_b3'], 'L1_gnn_W_msg': _L1_gnn_in['W_msg'], 'L1_gnn_b_msg': _L1_gnn_in['b_msg'], 'L1_gnn_W_ih': _L1_gnn_in['W_ih'], 'L1_gnn_W_hh': _L1_gnn_in['W_hh'], 'L1_gnn_b_ih': _L1_gnn_in['b_ih'], 'L1_gnn_b_hh': _L1_gnn_in['b_hh'], 'L2_gnn_W_in': _L2_gnn_in['W_in'], 'L2_gnn_W_out': _L2_gnn_in['W_out'], 'L3_gnn_Wq': _L3_gnn_in['Wq'], 'L3_gnn_bq': _L3_gnn_in['bq'], 'L3_gnn_Wk': _L3_gnn_in['Wk'], 'L3_gnn_bk': _L3_gnn_in['bk'], 'L3_gnn_Wv': _L3_gnn_in['Wv'], 'L3_gnn_bv': _L3_gnn_in['bv'], 'L3_gnn_Ws': _L3_gnn_in['Ws'], 'L3_gnn_bs': _L3_gnn_in['bs'], 'L3_gnn_Wb': _L3_gnn_in['Wb']}

def reference(x, adj, L0_gnn_v_node_feats, L0_gnn_uv_W1, L0_gnn_uv_b1, L0_gnn_uv_W2, L0_gnn_uv_b2, L0_gnn_uv_W3, L0_gnn_uv_b3, L0_gnn_vu_W1, L0_gnn_vu_b1, L0_gnn_vu_W2, L0_gnn_vu_b2, L0_gnn_vu_W3, L0_gnn_vu_b3, L1_gnn_W_msg, L1_gnn_b_msg, L1_gnn_W_ih, L1_gnn_W_hh, L1_gnn_b_ih, L1_gnn_b_hh, L2_gnn_W_in, L2_gnn_W_out, L3_gnn_Wq, L3_gnn_bq, L3_gnn_Wk, L3_gnn_bk, L3_gnn_Wv, L3_gnn_bv, L3_gnn_Ws, L3_gnn_bs, L3_gnn_Wb):
    import jax
    import jax.numpy as jnp

    def _L0_gnn_ref(u_node_feats, v_node_feats, uv_adj_mat, vu_adj_mat, uv_W1, uv_b1, uv_W2, uv_b2, uv_W3, uv_b3, vu_W1, vu_b1, vu_W2, vu_b2, vu_W3, vu_b3):
        import jax, jax.numpy as jnp
        import numpy as np
        NEG_SLOPE = 0.01
        N_U, N_V = (4096, 4096)
        U_F, V_F = (128, 128)
        HIDS = [128, 128]
        NUM_ROUNDS = 3

        def _glorot(key, fan_in, fan_out):
            lim = np.sqrt(6.0 / (fan_in + fan_out)).astype(np.float32)
            return jax.random.uniform(key, (fan_in, fan_out), jnp.float32, -lim, lim)

        def _mlp(x, W1, b1, W2, b2, W3, b3):
            a = jax.nn.leaky_relu
            x = a(x @ W1 + b1, NEG_SLOPE)
            x = a(x @ W2 + b2, NEG_SLOPE)
            return a(x @ W3 + b3, NEG_SLOPE)
        u, v = (u_node_feats, v_node_feats)
        for _ in range(NUM_ROUNDS):
            v = _mlp(uv_adj_mat @ u, uv_W1, uv_b1, uv_W2, uv_b2, uv_W3, uv_b3)
            u = _mlp(vu_adj_mat @ v, vu_W1, vu_b1, vu_W2, vu_b2, vu_W3, vu_b3)
        return v

    def _L1_gnn_ref(states, adj, W_msg, b_msg, W_ih, W_hh, b_ih, b_hh):
        import jax, jax.numpy as jnp
        import numpy as np
        N, DIM = (8192, 128)

        def _gru_cell(x, h, W_ih, W_hh, b_ih, b_hh):
            gi = x @ W_ih.T + b_ih
            gh = h @ W_hh.T + b_hh
            i_r, i_z, i_n = jnp.split(gi, 3, axis=-1)
            h_r, h_z, h_n = jnp.split(gh, 3, axis=-1)
            r = jax.nn.sigmoid(i_r + h_r)
            z = jax.nn.sigmoid(i_z + h_z)
            n = jnp.tanh(i_n + r * h_n)
            return (1.0 - z) * n + z * h
        agg = adj @ states
        msg = jax.nn.relu(agg @ W_msg.T + b_msg)
        return _gru_cell(msg, states, W_ih, W_hh, b_ih, b_hh)

    def _L2_gnn_ref(X, A, W_in, W_out):
        import jax, jax.numpy as jnp
        import numpy as np
        N = 8192
        IN_DIM = 128
        OUT_DIM = 128

        def _message(X, A, W):
            deg = jnp.sum(A, axis=1, keepdims=True)
            A_norm = A / jnp.where(deg > 0, deg, 1.0)
            return A_norm @ X @ W
        X_in = _message(X, A, W_in)
        X_out = _message(X, A.T, W_out)
        return X_in + X_out

    def _L3_gnn_ref(x, adj, Wq, bq, Wk, bk, Wv, bv, Ws, bs, Wb):
        import jax, jax.numpy as jnp
        import numpy as np
        N, IN, H, C = (2048, 128, 4, 32)
        HC = H * C
        EDGE_P = 0.008

        def _linear_params(key, fan_in, fan_out, bias=True):
            k1, k2 = jax.random.split(key)
            lim = 1.0 / np.sqrt(fan_in)
            W = jax.random.uniform(k1, (fan_in, fan_out), jnp.float32, -lim, lim)
            if not bias:
                return W
            b = jax.random.uniform(k2, (fan_out,), jnp.float32, -lim, lim)
            return (W, b)

        def _transformer_conv(x, adj, Wq, bq, Wk, bk, Wv, bv, Ws, bs, Wb):
            n = x.shape[0]
            q = (x @ Wq + bq).reshape(n, H, C)
            k = (x @ Wk + bk).reshape(n, H, C)
            v = (x @ Wv + bv).reshape(n, H, C)
            attn = jnp.einsum('nhc,mhc->hnm', q, k) / np.float32(np.sqrt(C))
            mask = adj == 0.0
            neg = jnp.where(mask[None], -jnp.inf, attn)
            m = jnp.max(neg, axis=-1, keepdims=True)
            all_inf = jnp.isneginf(m)
            e = jnp.where(mask[None], 0.0, jnp.exp(neg - jnp.where(all_inf, 0.0, m)))
            denom = jnp.sum(e, axis=-1, keepdims=True)
            alpha = e / jnp.where(denom == 0.0, 1.0, denom)
            out = jnp.einsum('hnm,mhc->hnc', alpha, v)
            out = jnp.transpose(out, (1, 2, 0)).reshape(n, C * H)
            x_r = x @ Ws + bs
            beta = jax.nn.sigmoid(jnp.concatenate([out, x_r, out - x_r], axis=-1) @ Wb)
            return beta * x_r + (1.0 - beta) * out
        return _transformer_conv(x, adj, Wq, bq, Wk, bk, Wv, bv, Ws, bs, Wb)
    x = _layernorm(x + _L0_gnn_ref(x, L0_gnn_v_node_feats, adj, adj, L0_gnn_uv_W1, L0_gnn_uv_b1, L0_gnn_uv_W2, L0_gnn_uv_b2, L0_gnn_uv_W3, L0_gnn_uv_b3, L0_gnn_vu_W1, L0_gnn_vu_b1, L0_gnn_vu_W2, L0_gnn_vu_b2, L0_gnn_vu_W3, L0_gnn_vu_b3), axis=-1)
    x = _layernorm(x + _L1_gnn_ref(x, adj, L1_gnn_W_msg, L1_gnn_b_msg, L1_gnn_W_ih, L1_gnn_W_hh, L1_gnn_b_ih, L1_gnn_b_hh), axis=-1)
    x = _layernorm(x + _L2_gnn_ref(x, adj, L2_gnn_W_in, L2_gnn_W_out), axis=-1)
    x = _layernorm(x + _L3_gnn_ref(x, adj, L3_gnn_Wq, L3_gnn_bq, L3_gnn_Wk, L3_gnn_bk, L3_gnn_Wv, L3_gnn_bv, L3_gnn_Ws, L3_gnn_bs, L3_gnn_Wb), axis=-1)
    return x

_drawn_inputs = setup_inputs


def setup_inputs(seed=0):
    import zlib

    import numpy as np

    out = dict(_drawn_inputs(seed))
    spreads = {'L0_gnn_uv_b1': (0.0, 0.1),
     'L0_gnn_uv_b2': (0.0, 0.1),
     'L0_gnn_uv_b3': (0.0, 0.1),
     'L0_gnn_vu_b1': (0.0, 0.1),
     'L0_gnn_vu_b2': (0.0, 0.275),
     'L0_gnn_vu_b3': (0.0, 0.1)}
    factors = {'L1_gnn_b_msg': 8.0,
     'L1_gnn_b_ih': 2.764,
     'L1_gnn_b_hh': 5.105,
     'L3_gnn_Wq': 3.145,
     'L3_gnn_bq': 8.0,
     'L3_gnn_Wk': 2.843,
     'L3_gnn_bk': 8.0}
    for name, (base, spread) in spreads.items():
        noise = np.random.default_rng([zlib.crc32(name.encode()), seed]).standard_normal(out[name].shape)
        drawn = base * np.exp(spread * noise) if base else spread * noise
        out[name] = jnp.asarray(drawn.astype(out[name].dtype))
    for name, factor in factors.items():
        out[name] = (out[name] * factor).astype(out[name].dtype)
    return out
```

```python
import concourse.bass as bass
from concourse import mybir
from contextlib import ExitStack

F32 = mybir.dt.float32
F32R = mybir.dt.float32r
BF16 = mybir.dt.bfloat16
ALU = mybir.AluOpType
ACT = mybir.ActivationFunctionType
AX = mybir.AxisListType

P = 128
N = 4096
D = 128
NT = N // P
HALF = 2048
BANK = 512
NB = HALF // BANK
PAIR = 2 * BANK
PT = PAIR // P
RING = 4
X_FIRST = 4
TAIL_TILES = 16
STEPS = 6
GRU_STEPS = 9
PRODUCTS = 8
HALVES = 2 * PRODUCTS
EPS = 1e-5
SLOPE = 0.01
HEADS = 4
C = D // HEADS
CHUNK = 512
NC = N // CHUNK
QT = CHUNK // P
KC = N // CHUNK
BIG = 1e30

(UV1, UV2, UV3, VU1, VU2, VU3, WMSG, WIR, WIZ, WIN, WHR, WHZ, WHN, LIN, LOUT) = range(15)
(BUV1, BUV2, BVU1, BVU2, BMSG, BIR, BIZ, BIN, BHR, BHZ, BHN, BS) = range(12)
(RUV3, RVU3, RBV) = range(3)


def at_least(engine, semaphore, value):
    if isinstance(value, int) and value <= 0:
        return
    engine.wait_ge(semaphore, value)


class Chain:

    def __init__(self, engine, semaphore):
        self.engine, self.semaphore, self.count = engine, semaphore, 0

    def link(self, instruction):
        instruction.then_inc(self.semaphore, 1)
        self.count = self.count + 1
        self.engine.wait_ge(self.semaphore, self.count)


def graph_kernel(nc, x, adj, adj_t, weights, bias_cols, bias_rows, wq_rep, wk_rep, bq_rep, bk_rep,
                 wv, ws_perm, wb_cols, out):
    ctx = ExitStack()
    with ctx:
        def sb(name, shape, dt=F32, where=ctx):
            return where.enter_context(nc.sbuf_tensor(name, shape, dt))

        def sem(name):
            return ctx.enter_context(nc.semaphore(name))

        psum = ctx.enter_context(nc.psum_tensor("psum", [P, 8 * BANK], F32))

        V = sb("V", [P, NT, D])
        ident = sb("ident", [P, P])
        ident_b = sb("ident_b", [P, P], BF16)
        ones = sb("ones", [P, C])
        minus_half = sb("minus_half", [P, PT])
        rows = sb("rows", [P, 3, D])
        wq_sb = sb("wq_sb", [P, HEADS, 3 * C])
        wk_sb = sb("wk_sb", [P, HEADS, 3 * C])
        bq_sb = sb("bq_sb", [3 * C, HEADS])
        bk_sb = sb("bk_sb", [3 * C, HEADS])
        wv_sb = sb("wv_sb", [P, D])
        ws_sb = sb("ws_sb", [P, D])
        wb_sb = sb("wb_sb", [P, 3])
        cols = sb("cols", [P, 12])
        norm_stats = sb("norm_stats", [P, PT, 6])
        norm_mv = sb("norm_mv", [P, PT, 2])
        norm_ve = sb("norm_ve", [P, PT])
        norm_rstd = sb("norm_rstd", [P, PT])

        consts_in = sem("consts_in")
        setup_pool = sem("setup_pool")
        setup_dve = sem("setup_dve")
        dve_chain = sem("dve_chain")
        pool_chain = sem("pool_chain")
        variance_ready = sem("variance_ready")
        rstd_ready = sem("rstd_ready")

        def norm_begin(chain, count, src):
            for t in range(count):
                last = nc.vector.bn_stats(norm_stats[:, t, :], src[:, t, :])
            chain.link(last)
            for t in range(count):
                last = nc.vector.bn_aggr(norm_mv[:, t, :], norm_stats[:, t, :])
            chain.link(last)
            nc.vector.tensor_scalar(norm_ve[:, 0:count], norm_mv[:, 0:count, 1], EPS, None, ALU.add)\
                .then_inc(variance_ready, 1)

        def norm_end(dve, i, count, dst, src):
            dve.wait_ge(rstd_ready, i + 1)
            for t in range(count):
                last = nc.vector.tensor_scalar(dst[:, t, :], src[:, t, :], norm_mv[:, t, 0:1],
                                               norm_rstd[:, t:t + 1], ALU.subtract, ALU.mult)
            return last

        part = ExitStack()
        with part:
            U = sb("U", [P, NT, D], where=part)
            X0 = sb("X0", [P, NT, D], where=part)
            w_sb = sb("w_sb", [P, 15, D], where=part)
            raw = sb("raw", [P, RING, HALF], where=part)
            adj_hi = sb("adj_hi", [P, RING, HALF], F32R, where=part)
            adj_lo = sb("adj_lo", [P, RING, HALF], F32R, where=part)
            x_hi = sb("x_hi", [P, RING, D], F32R, where=part)
            x_lo = sb("x_lo", [P, RING, D], F32R, where=part)
            agg = sb("agg", [P, 2, PAIR], where=part)
            act1 = sb("act1", [P, PAIR], where=part)
            act2 = sb("act2", [P, PAIR], where=part)
            pre = sb("pre", [P, PAIR], where=part)
            gate_r = sb("gate_r", [P, PAIR], where=part)
            gate_z = sb("gate_z", [P, PAIR], where=part)
            cand = sb("cand", [P, PAIR], where=part)
            gate_bias = sb("gate_bias", [P, 2], where=part)
            col_parts = sb("col_parts", [P, 2, NT], where=part)
            row_parts = sb("row_parts", [P, 2, NT], where=part)
            inv_col_deg = sb("inv_col_deg", [P, NT], where=part)
            inv_row_deg = sb("inv_row_deg", [P, NT], where=part)
            deg_flag = sb("deg_flag", [P, NT], where=part)

            in_buf = [X0, V, U, V, U, V, U, U]
            out_buf = [V, U, V, U, V, U, X0, V]
            MLP = {0: (UV1, BUV1, RUV3), 1: (VU1, BVU1, RVU3), 2: (UV1, BUV1, RUV3),
                   3: (VU1, BVU1, RVU3), 4: (UV1, BUV1, RUV3)}
            GRU, CONV_T, CONV = 5, 6, 7
            NORMED = [4, GRU, CONV]

            x_in = sem("x_in")
            x_rest_in = sem("x_rest_in")
            raw_in = [sem(f"raw_in{s}") for s in range(RING)]
            hi_ready = sem("hi_ready")
            lo_ready = sem("lo_ready")
            stage_ready = sem("stage_ready")
            stage_hi = sem("stage_hi")
            tile_used = sem("tile_used")
            agg_ready = sem("agg_ready")
            layer1_done = sem("layer1_done")
            layer2_done = sem("layer2_done")
            layer3_done = sem("layer3_done")
            sum1_ready = sem("sum1_ready")
            sum2_ready = sem("sum2_ready")
            act1_ready = sem("act1_ready")
            act2_ready = sem("act2_ready")
            pre_ready = sem("pre_ready")
            mlp_ready = sem("mlp_ready")
            norm_ready = sem("norm_ready")
            msg_done = sem("msg_done")
            msg_ready = sem("msg_ready")
            gates_done = sem("gates_done")
            gates_tanh = sem("gates_tanh")
            gates_ready = sem("gates_ready")
            cand_done = sem("cand_done")
            cand_pre = sem("cand_pre")
            cand_ready = sem("cand_ready")
            state_ready = sem("state_ready")
            state_done = sem("state_done")
            conv_done = sem("conv_done")
            conv_ready = sem("conv_ready")

            def accumulator(half, bank):
                q = 4 * (half % 2) + bank
                return psum[:, q * BANK:(q + 1) * BANK]

            def scratch(half, which):
                q = 4 * (half % 2) + 2 * which
                return psum[:, q * BANK:(q + 2) * BANK]

            def per_tile(ap):
                return ap.rearrange("p (t d) -> p t d", d=D)

            def pair_of(buf, half, k):
                t0 = (half % 2) * (HALF // P) + k * PT
                return buf[:, t0:t0 + PT, :]

            def whole(product):
                return product in (GRU, CONV_T)

            def tail_steps(tail, h, hs, n):
                if hs > 0:
                    last = (hs - 1) // 2
                    for k in range(2):
                        tail(h, hs - 1, last, k, n - k * (GRU_STEPS if last == GRU else STEPS))

            def halves(engine, half_body, constants):
                half_body(0, 0)
                constants()
                with engine.Fori(0, 2) as r:
                    for hs in range(1, 5):
                        half_body(hs + 4 * r, hs)
                for h in range(9, HALVES):
                    half_body(h, h)

            def tiles(engine, hs, tile_body, tail_body):
                for n in range(TAIL_TILES):
                    tile_body(n, n, n // RING)
                    tail_body(n)
                if whole(hs // 2):
                    for n in range(TAIL_TILES, NT):
                        tile_body(n, n, n // RING)
                        tail_body(n)
                else:
                    with engine.Fori(TAIL_TILES // RING, NT // RING - 1) as g:
                        for s in range(RING):
                            tile_body(RING * g + s, TAIL_TILES + s, g)
                    for n in range(NT - RING, NT):
                        tile_body(n, n, n // RING)

            with nc.Block() as block:

                @block.sync
                def _(sp):
                    x_tiles = x.rearrange("(t p) d -> p t d", p=P)
                    sp.dma_start(X0[:, 0:X_FIRST, :], x_tiles[:, 0:X_FIRST, :]).then_inc(x_in, 16)

                    def half_body(h, hs):
                        source = adj if hs // 2 == CONV_T else adj_t
                        c0 = (hs % 2) * HALF

                        def load(n, s, g):
                            at_least(sp, lo_ready, NT * h + n - RING + 1)
                            if isinstance(n, int):
                                src = source[n * P:(n + 1) * P, c0:c0 + HALF]
                            else:
                                src = source[bass.ds(n * P, P), c0:c0 + HALF]
                            sp.dma_start(raw[:, s % RING, :], src).then_inc(raw_in[s % RING], 16)

                        def rest_of_x(n):
                            if hs == 0 and n == 1:
                                sp.dma_start(X0[:, X_FIRST:NT, :], x_tiles[:, X_FIRST:NT, :])\
                                    .then_inc(x_rest_in, 16)

                        tiles(sp, hs, load, rest_of_x)

                    halves(sp, half_body, lambda: None)

                @block.gpsimd
                def _(pool):
                    pool.memset(ident[:, :], 0.0).then_inc(setup_pool, 1)
                    pool.memset(ident_b[:, :], 0.0).then_inc(setup_pool, 1)
                    pool.memset(ones[:, :], 1.0).then_inc(setup_pool, 1)
                    pool.memset(minus_half[:, :], -0.5).then_inc(setup_pool, 1)
                    pool.wait_ge(setup_pool, 4)
                    for m in (ident, ident_b):
                        pool.affine_select(out=m[:, :], in_=m[:, :], compare_op=ALU.not_equal, fill=1.0,
                                           base=0, pattern=[[-1, P]], channel_multiplier=1)\
                            .then_inc(setup_pool, 1)
                    pool.wait_ge(x_in, 16)
                    pool.wait_ge(setup_pool, 6)

                    def stage(h, n):
                        product, first_half = h // 2, h % 2 == 0
                        source = in_buf[product]
                        if first_half and product > 0 and n % PT == 0:
                            pairs = 2 * (n // PT + 1)
                            if product < GRU:
                                pool.wait_ge(mlp_ready, 4 * (h - 2) + pairs)
                            elif product == GRU:
                                pool.wait_ge(norm_ready, pairs)
                            elif product == CONV_T:
                                pool.wait_ge(norm_ready, 8 + pairs)
                        if h == 0 and n == X_FIRST:
                            pool.wait_ge(x_rest_in, 16)
                        at_least(pool, tile_used, NT * h + n + 2 - RING)
                        slots = slice(n % RING, n % RING + 2)
                        pool.tensor_copy(x_hi[:, slots, :], source[:, n:n + 2, :]).then_inc(stage_hi, 1)
                        pool.wait_ge(stage_hi, (NT * h + n) // 2 + 1)
                        pool.tensor_tensor(x_lo[:, slots, :], source[:, n:n + 2, :],
                                           x_hi[:, slots, :].bitcast(F32), ALU.subtract)\
                            .then_inc(stage_ready, 2)

                    def rsqrt(i):
                        pool.wait_ge(variance_ready, i + 1)
                        pool.tensor_tensor(norm_rstd[:, :], norm_ve[:, :], minus_half[:, :], ALU.pow)\
                            .then_inc(rstd_ready, 1)

                    for h in range(HALVES):
                        for n in range(0, NT, 2):
                            stage(h, n)
                            last = (h - 1) // 2
                            at = {4: (8, 14), GRU: (10, 20), CONV: (4, 10)}.get(last)
                            if last in NORMED and n in at:
                                rsqrt(4 * NORMED.index(last) + 2 * ((h - 1) % 2) + at.index(n))
                    for k in range(2):
                        rsqrt(4 * NORMED.index(CONV) + 2 + k)

                @block.scalar
                def _(act):
                    def load_constants():
                        act.dma_start(w_sb[:, :, :], weights).then_inc(consts_in, 16)
                        act.dma_start(cols[:, :], bias_cols).then_inc(consts_in, 16)
                        for r in range(3):
                            act.dma_start(rows[:, r, :], bias_rows[r].partition_broadcast(P)).then_inc(consts_in, 16)
                        for dst, src in ((wq_sb[:, :, :], wq_rep), (wk_sb[:, :, :], wk_rep), (bq_sb[:, :], bq_rep),
                                         (bk_sb[:, :], bk_rep), (wv_sb[:, :], wv), (ws_sb[:, :], ws_perm),
                                         (wb_sb[:, :], wb_cols)):
                            act.dma_start(dst, src).then_inc(consts_in, 16)

                    def half_body(h, hs):
                        product = hs // 2

                        def make_hi(n, s, g):
                            slot = s % RING
                            act.wait_ge(raw_in[slot], 16 * ((NT // RING) * h + g + 1))
                            at_least(act, tile_used, NT * h + n - RING + 1)
                            sums = {}
                            if whole(product):
                                parts = col_parts if product == GRU else row_parts
                                sums = dict(accum_out=parts[:, hs % 2, n:n + 1])
                            act.activation(adj_hi[:, slot, :], raw[:, slot, :], ACT.Copy, **sums)\
                                .then_inc(hi_ready, 1)

                        def after(n):
                            if hs == 0 and n == RING:
                                load_constants()
                            if hs > 0 and n in (3, 4):
                                act.wait_ge(tile_used, NT * h)
                                act.activation(agg[:, n - 3, :], scratch(hs - 1, n - 3), ACT.Copy)\
                                    .then_inc(agg_ready, 1)
                            tail_steps(tail, h, hs, n)

                        tiles(act, hs, make_hi, after)

                    def tail(h, before, last, k, step):
                        pair = 2 * (h - 1) + k
                        if last <= 4:
                            b1 = MLP[last][1]
                            if step == 4:
                                act.wait_ge(layer1_done, pair + 1)
                                act.activation(act1[:, :], scratch(before, k), ACT.Identity,
                                               bias=cols[:, b1:b1 + 1]).then_inc(sum1_ready, 1)
                            if step == 6:
                                act.wait_ge(layer2_done, pair + 1)
                                act.activation(act2[:, :], scratch(before, k), ACT.Identity,
                                               bias=cols[:, b1 + 1:b1 + 2]).then_inc(sum2_ready, 1)
                        if last == GRU:
                            i = pair - 4 * GRU
                            if step == 4:
                                act.wait_ge(msg_done, i + 1)
                                act.activation(act1[:, :], scratch(before, 0), ACT.Relu,
                                               bias=cols[:, BMSG:BMSG + 1]).then_inc(msg_ready, 1)
                                act.activation(act2[:, :], scratch(before, 1), ACT.Copy).then_inc(msg_ready, 1)
                            for j, gate in enumerate((gate_r, gate_z)):
                                if step == 6 + j:
                                    act.wait_ge(gates_done, 2 * i + j + 1)
                                    act.activation(gate[:, :], scratch(before, j), ACT.Tanh, scale=0.5,
                                                   bias=gate_bias[:, j:j + 1]).then_inc(gates_tanh, 1)
                                    act.wait_ge(gates_tanh, 2 * i + j + 1)
                                    act.activation(gate[:, :], gate[:, :], ACT.Copy, scale=0.5, bias=0.5)\
                                        .then_inc(gates_ready, 1)
                            if step == 9:
                                act.wait_ge(cand_pre, i + 1)
                                act.activation(cand[:, :], pre[:, :], ACT.Tanh).then_inc(cand_ready, 1)

                    def constants():
                        act.wait_ge(consts_in, 16 * 12)
                        act.wait_ge(setup_dve, 2)

                    halves(act, half_body, constants)
                    for k in range(2):
                        act.wait_ge(tile_used, NT * HALVES)
                        act.activation(agg[:, k, :], scratch(HALVES - 1, k), ACT.Copy).then_inc(agg_ready, 1)
                    for n in range(TAIL_TILES):
                        tail_steps(tail, HALVES, HALVES, n)

                @block.tensor
                def _(pe):

                    def half_body(h, hs):
                        def multiply(n, s, g):
                            slot = s % RING
                            at = NT * h + n
                            first, final = s == 0, s == NT - 1
                            if first and hs >= 2:
                                done = (hs - 2) // 2
                                if done <= 4:
                                    pe.wait_ge(pre_ready, 2 * (h - 1))
                                elif done == GRU:
                                    pe.wait_ge(norm_ready, 2 * 2 * (h - 1) - 2 * 4 * 4)
                                else:
                                    pe.wait_ge(conv_ready, 2 * (h - 1) - 4 * CONV_T)
                            if s % 2 == 0:
                                pe.wait_ge(stage_ready, at + 2)
                            pe.wait_ge(hi_ready, at + 1)
                            for b in range(NB):
                                nc.tensor.matmul(accumulator(hs, b), x_hi[:, slot, :],
                                                 adj_hi[:, slot, b * BANK:(b + 1) * BANK], start=first, stop=False)
                            for b in range(NB):
                                nc.tensor.matmul(accumulator(hs, b), x_lo[:, slot, :],
                                                 adj_hi[:, slot, b * BANK:(b + 1) * BANK], start=False, stop=False)
                            pe.wait_ge(lo_ready, at + 1)
                            for b in range(NB):
                                mm = nc.tensor.matmul(accumulator(hs, b), x_hi[:, slot, :],
                                                      adj_lo[:, slot, b * BANK:(b + 1) * BANK],
                                                      start=False, stop=final)
                            mm.then_inc(tile_used, 1)

                        tiles(pe, hs, multiply, lambda n: tail_steps(tail, h, hs, n))

                    def dense(out_, w, rhs, start=True, stop=True):
                        for b in range(2):
                            mm = nc.tensor.matmul(out_[:, b * BANK:(b + 1) * BANK], w_sb[:, w, :],
                                                  rhs[:, b * BANK:(b + 1) * BANK], start=start, stop=stop)
                        return mm

                    def dense_to_rows(out_, lhs, w):
                        for t in range(PT):
                            mm = nc.tensor.matmul(out_[:, t * D:(t + 1) * D], lhs[:, t * P:(t + 1) * P],
                                                  w_sb[:, w, :], start=True, stop=True)
                        return mm

                    def tail(h, before, last, k, step):
                        pair = 2 * (h - 1) + k
                        if last <= 4:
                            w1 = MLP[last][0]
                            if step == 1:
                                pe.wait_ge(agg_ready, pair + 1)
                                dense(scratch(before, k), w1, agg[:, k, :]).then_inc(layer1_done, 1)
                            if step == 3:
                                pe.wait_ge(act1_ready, pair + 1)
                                dense(scratch(before, k), w1 + 1, act1[:, :]).then_inc(layer2_done, 1)
                            if step == 5:
                                pe.wait_ge(act2_ready, pair + 1)
                                dense_to_rows(scratch(before, k), act2[:, :], w1 + 2).then_inc(layer3_done, 1)
                        if last == GRU:
                            i = pair - 4 * GRU
                            if step == 2:
                                pe.wait_ge(agg_ready, 2 * h)
                                if k == 1:
                                    pe.wait_ge(norm_ready, 8 + 2 * i)
                                dense(scratch(before, 0), WMSG, agg[:, k, :])
                                old = pair_of(in_buf[last], before, k)
                                for t in range(PT):
                                    mm = nc.tensor.transpose(scratch(before, 1)[:, t * P:(t + 1) * P],
                                                             old[:, t, :], ident[:, :])
                                mm.then_inc(msg_done, 1)
                            if step in (4, 5):
                                pe.wait_ge(msg_ready, 2 * i + 2)
                                wi, wh = ((WIR, WHR), (WIZ, WHZ))[step - 4]
                                dense(scratch(before, step - 4), wi, act1[:, :], stop=False)
                                dense(scratch(before, step - 4), wh, act2[:, :], start=False)\
                                    .then_inc(gates_done, 1)
                            if step == 7:
                                pe.wait_ge(gates_tanh, 2 * i + 2)
                                dense(scratch(before, 0), WHN, act2[:, :])
                                dense(scratch(before, 1), WIN, act1[:, :]).then_inc(cand_done, 1)
                            if step == 9:
                                pe.wait_ge(state_ready, i + 1)
                                for t in range(PT):
                                    mm = nc.tensor.transpose(scratch(before, 0)[:, t * D:(t + 1) * D],
                                                             gate_z[:, t * P:(t + 1) * P], ident[:, :])
                                mm.then_inc(state_done, 1)
                        if last in (CONV_T, CONV) and step == 1:
                            pe.wait_ge(agg_ready, pair + 1)
                            dense_to_rows(scratch(before, k), agg[:, k, :],
                                          LOUT if last == CONV_T else LIN).then_inc(conv_done, 1)

                    def constants():
                        pe.wait_ge(consts_in, 16 * 12)
                        pe.wait_ge(setup_pool, 6)

                    halves(pe, half_body, constants)
                    for n in range(TAIL_TILES):
                        tail_steps(tail, HALVES, HALVES, n)

                @block.vector
                def _(dve):
                    chain = Chain(dve, dve_chain)

                    def constants():
                        dve.wait_ge(consts_in, 16 * 12)
                        for g, (bi, bh) in enumerate(((BIR, BHR), (BIZ, BHZ))):
                            chain.link(nc.vector.tensor_tensor(gate_bias[:, g:g + 1], cols[:, bi:bi + 1],
                                                               cols[:, bh:bh + 1], ALU.add))
                            nc.vector.tensor_scalar(gate_bias[:, g:g + 1], gate_bias[:, g:g + 1], 0.5, None,
                                                    ALU.mult).then_inc(setup_dve, 1)

                    def half_body(h, hs):
                        def make_lo(n, s, g):
                            slot = s % RING
                            dve.wait_ge(hi_ready, NT * h + n + 1)
                            nc.vector.tensor_tensor(adj_lo[:, slot, :], raw[:, slot, :],
                                                    adj_hi[:, slot, :].bitcast(F32), ALU.subtract)\
                                .then_inc(lo_ready, 1)

                        def after(n):
                            if n == 1 and hs in (2 * CONV_T, 2 * CONV):
                                degrees(*((col_parts, inv_col_deg) if hs == 2 * CONV_T
                                          else (row_parts, inv_row_deg)))
                            tail_steps(tail, h, hs, n)

                        tiles(dve, hs, make_lo, after)

                    def leaky(dst, src):
                        return nc.vector.scalar_tensor_tensor(dst, src, SLOPE, src, op0=ALU.mult, op1=ALU.max)

                    def degrees(parts, inverse):
                        chain.link(nc.vector.tensor_tensor(inverse[:, :], parts[:, 0, :], parts[:, 1, :], ALU.add))
                        chain.link(nc.vector.tensor_scalar(deg_flag[:, :], inverse[:, :], 0.0, None, ALU.is_gt))
                        chain.link(nc.vector.tensor_tensor(inverse[:, :], inverse[:, :], deg_flag[:, :], ALU.mult))
                        chain.link(nc.vector.tensor_scalar(deg_flag[:, :], deg_flag[:, :], -1.0, 1.0,
                                                           ALU.mult, ALU.add))
                        chain.link(nc.vector.tensor_tensor(inverse[:, :], inverse[:, :], deg_flag[:, :], ALU.add))
                        chain.link(nc.vector.reciprocal(inverse[:, :], inverse[:, :]))

                    def tail(h, before, last, k, step):
                        pair = 2 * (h - 1) + k
                        if last < GRU and step == 4:
                            dve.wait_ge(sum1_ready, pair + 1)
                            leaky(act1[:, :], act1[:, :]).then_inc(act1_ready, 1)
                        if last < GRU and step == 6:
                            dve.wait_ge(sum2_ready, pair + 1)
                            leaky(act2[:, :], act2[:, :]).then_inc(act2_ready, 1)
                        if last < GRU and step == 8:
                            dve.wait_ge(layer3_done, pair + 1)
                            r3 = MLP[last][2]
                            nc.vector.tensor_tensor(
                                per_tile(pre[:, :]), per_tile(scratch(before, k)),
                                rows[:, r3:r3 + 1, :].broadcast_to([P, PT, D]), ALU.add).then_inc(pre_ready, 1)
                            dve.wait_ge(pre_ready, pair + 1)
                            dst = pair_of(out_buf[last], before, k) if last < 4 else per_tile(cand[:, :])
                            leaky(dst, per_tile(pre[:, :])).then_inc(mlp_ready, 2)
                        if last == 4 and step == 8:
                            dve.wait_ge(mlp_ready, 2 * pair + 2)
                            chain.link(nc.vector.tensor_tensor(per_tile(cand[:, :]), per_tile(cand[:, :]),
                                                               pair_of(X0, before, k), ALU.add))
                            norm_begin(chain, PT, per_tile(cand[:, :]))
                        if last == 4 and step == 9:
                            norm_end(dve, pair - 16, PT, pair_of(out_buf[last], before, k),
                                     per_tile(cand[:, :])).then_inc(norm_ready, 2)
                        if last == GRU:
                            i = pair - 4 * GRU
                            if step == 9:
                                dve.wait_ge(cand_done, i + 1)
                                dve.wait_ge(gates_ready, 2 * i + 2)
                                chain.link(nc.vector.scalar_tensor_tensor(
                                    pre[:, :], scratch(before, 0), cols[:, BHN:BHN + 1], gate_r[:, :],
                                    op0=ALU.add, op1=ALU.mult))
                                nc.vector.scalar_tensor_tensor(
                                    pre[:, :], scratch(before, 1), cols[:, BIN:BIN + 1], pre[:, :],
                                    op0=ALU.add, op1=ALU.add).then_inc(cand_pre, 1)
                            if step == 10:
                                dve.wait_ge(cand_ready, i + 1)
                                chain.link(nc.vector.tensor_tensor(act2[:, :], act2[:, :], cand[:, :], ALU.subtract))
                                chain.link(nc.vector.tensor_tensor(act2[:, :], act2[:, :], gate_z[:, :], ALU.mult))
                                nc.vector.tensor_tensor(gate_z[:, :], act2[:, :], cand[:, :], ALU.add)\
                                    .then_inc(state_ready, 1)
                            if step == 11:
                                dve.wait_ge(state_done, i + 1)
                                old = pair_of(in_buf[last], before, k)
                                chain.link(nc.vector.tensor_tensor(per_tile(pre[:, :]), per_tile(scratch(before, 0)),
                                                                   old, ALU.add))
                                norm_begin(chain, PT, per_tile(pre[:, :]))
                            if step == 12:
                                norm_end(dve, 4 + i, PT, pair_of(out_buf[last], before, k),
                                         per_tile(pre[:, :])).then_inc(norm_ready, 2)
                        if last in (CONV_T, CONV) and step == 4:
                            i = pair - 4 * CONV_T
                            dve.wait_ge(conv_done, i + 1)
                            t0 = (before % 2) * (HALF // P) + k * PT
                            inverse = inv_col_deg if last == CONV_T else inv_row_deg
                            dst = pair_of(X0, before, k) if last == CONV_T else per_tile(pre[:, :])
                            if last == CONV:
                                dve.wait_ge(norm_ready, 16 + 2 * (i - 4))
                            nc.vector.tensor_tensor(
                                dst, per_tile(scratch(before, k)),
                                inverse[:, t0:t0 + PT].rearrange("p (t o) -> p t o", o=1).broadcast_to([P, PT, D]),
                                ALU.mult).then_inc(conv_ready, 1)
                            if last == CONV:
                                dve.wait_ge(conv_ready, i + 1)
                                for other in (X0, U):
                                    chain.link(nc.vector.tensor_tensor(
                                        per_tile(pre[:, :]), per_tile(pre[:, :]), pair_of(other, before, k), ALU.add))
                                norm_begin(chain, PT, per_tile(pre[:, :]))
                        if last == CONV and step == 5:
                            norm_end(dve, 4 + pair - 4 * CONV_T, PT, pair_of(V, before, k),
                                     per_tile(pre[:, :])).then_inc(norm_ready, 2)

                    halves(dve, half_body, constants)
                    for n in range(TAIL_TILES):
                        tail_steps(tail, HALVES, HALVES, n)

        K = sb("K", [P, HEADS, N], F32R)
        QA = sb("QA", [P, HEADS, CHUNK], F32R)
        QB = sb("QB", [P, HEADS, CHUNK], F32R)
        XT = sb("XT", [P, N])
        values = sb("values", [P, NT, D])
        raw_t = sb("raw_t", [P, 2, 2, CHUNK])
        mask_t = sb("mask_t", [P, 2, 2, CHUNK], BF16)
        raw_q = sb("raw_q", [P, 2, 2 * CHUNK])
        mask_q = sb("mask_q", [P, 2, N], BF16)
        masked = sb("masked", [P, 4, CHUNK], BF16)
        maxima = sb("maxima", [P, HEADS, KC])
        row_max = sb("row_max", [P, HEADS])
        minus_hi = sb("minus_hi", [P, HEADS], F32R)
        spread = sb("spread", [P, HEADS, 98])
        E = sb("E", [P, 4, 2 * CHUNK])
        wb_rep = sb("wb_rep", [P, 2, P])
        xc = sb("xc", [P, QT, D])
        denom = sb("denom", [P, CHUNK])
        att = sb("att", [P, CHUNK])
        xr = sb("xr", [P, CHUNK])
        beta = sb("beta", [P, CHUNK])
        mixed = sb("mixed", [P, CHUNK])
        y = sb("y", [P, QT, D])

        xc_ready = sem("xc_ready")
        xt_stored = sem("xt_stored")
        xc_turned = sem("xc_turned")
        xct_ready = sem("xct_ready")
        keys_done = sem("keys_done")
        keys_hi = sem("keys_hi")
        keys_split = sem("keys_split")
        values_done = sem("values_done")
        values_ready = sem("values_ready")
        head_setup = sem("head_setup")
        raw_t_in = [sem(f"raw_t_in{s}") for s in range(2)]
        raw_q_in = [sem(f"raw_q_in{s}") for s in range(2)]
        mask_t_ready = sem("mask_t_ready")
        mask_q_ready = sem("mask_q_ready")
        side_done = sem("side_done")
        side_read = sem("side_read")
        spread_ready = sem("spread_ready")
        queries_ready = sem("queries_ready")
        scores_done = sem("scores_done")
        exp_done = sem("exp_done")
        summed = sem("summed")
        sums_read = sem("sums_read")
        att_ready = sem("att_ready")
        part2_chain = sem("part2_chain")
        query_hi = sem("query_hi")
        gate_tanh = sem("gate_tanh")
        gate_ready = sem("gate_ready")
        mixed_ready = sem("mixed_ready")
        y_ready = sem("y_ready")
        y_out = sem("y_out")

        PREP = HEADS + QT * (HEADS * KC + 1)
        FINISH = 4
        assert PREP % 2 == 0 and FINISH % 2 == 0

        DIVIDE_AT, XR_AT, LOGIT_AT, GATE_AT, MIX_AT, TURN_AT, NORM_AT = 2, 3, 5, 6, 8, 10, 12

        def bank(b):
            return psum[:, b * BANK:(b + 1) * BANK]

        def score_banks(hp):
            return psum[:, 2 * hp * BANK:2 * (hp + 1) * BANK]

        OUT_BANK, DEN_BANK, SIDE_BANKS = 4, 5, 6

        def side_order(with_prep, with_finish):
            order = [[] for _ in range(NT)]
            if with_prep:
                order[0] += [("query", h) for h in range(HEADS)]
            if with_finish:
                order[XR_AT] += [("xr",)]
                order[LOGIT_AT] += [("logit",)]
                order[TURN_AT] += [("turn", 0), ("turn", 1)]
            if with_prep:
                rest = []
                for t in range(QT):
                    for u, (h, kc) in enumerate((h, kc) for h in range(HEADS) for kc in range(KC)):
                        rest.append(("score", t, h, kc))
                        if t > 0 and u == 7:
                            rest.append(("maximum", t - 1))
                t = 1
                while rest:
                    count = {1: 4, DIVIDE_AT: 2, XR_AT: 4, LOGIT_AT: 4, MIX_AT: 3, TURN_AT: 2, NORM_AT: 3}.get(t, 5)
                    order[t] += rest[:count]
                    rest, t = rest[count:], t + 1
                assert t < NT
                order[t] += [("maximum", QT - 1)]
            return order

        def side_base(c):
            if isinstance(c, int) and c == 0:
                return PREP
            return (PREP - FINISH) + (PREP + FINISH) * c

        def logit_at(with_prep):
            return [item for items in side_order(with_prep, True) for item in items].index(("logit",))

        with nc.Block() as block:

            @block.sync
            def _(sp):
                def load_t(c, j):
                    at_least(sp, mask_t_ready, (NT // 2) * c + j - 1)
                    cols_ = slice(c * CHUNK, (c + 1) * CHUNK) if isinstance(c, int) else bass.ds(c * CHUNK, CHUNK)
                    src = adj_t.rearrange("(t p) n -> p t n", p=P)[:, 2 * j:2 * j + 2, cols_]
                    sp.dma_start(raw_t[:, j % 2, :, :], src).then_inc(raw_t_in[j % 2], 16)

                def load_q(c, t, quarter):
                    at_least(sp, mask_q_ready, 4 * (QT * c + t) + quarter - 1)
                    row = (QT * c + t) * P
                    rows_ = slice(row, row + P) if isinstance(c, int) else bass.ds(row, P)
                    sp.dma_start(raw_q[:, quarter % 2, :], adj[rows_, quarter * 2 * CHUNK:(quarter + 1) * 2 * CHUNK])\
                        .then_inc(raw_q_in[quarter % 2], 16)

                def body(c, with_prep, with_finish, more=True):
                    order = side_order(with_prep, with_finish)
                    for t in range(NT):
                        if t % 2 == 0 and t + 2 < NT:
                            load_t(c, t // 2 + 1)
                        elif t % 2 == 0 and with_prep:
                            load_t(c + 1, 0)
                        for item in order[t]:
                            if item[0] == "score" and item[3] == KC - 1:
                                if item[1] + 1 < QT:
                                    load_q(c + 1, item[1] + 1, item[2])
                                elif more:
                                    load_q(c + 2, 0, item[2])
                        if with_finish and t == 16:
                            store(c - 1)

                def store(c):
                    rows_ = slice(c * CHUNK, (c + 1) * CHUNK) if isinstance(c, int) else bass.ds(c * CHUNK, CHUNK)
                    sp.wait_ge(y_ready, c + 1)
                    sp.dma_start(out[rows_, :].rearrange("(t p) d -> p t d", p=P), y[:, :, :]).then_inc(y_out, 16)

                for t in range(QT):
                    for quarter in range(4):
                        load_q(0, t, quarter)
                for quarter in range(4):
                    load_q(1, 0, quarter)
                load_t(0, 0)
                body(0, True, False)
                with sp.Fori(1, NC - 2) as c:
                    body(c, True, True)
                body(NC - 2, True, True, more=False)
                body(NC - 1, False, True)
                store(NC - 1)
                sp.wait_ge(y_out, 16 * NC)

            @block.gpsimd
            def _(pool):
                pool.memset(spread[:, :, :], 0.0).then_inc(setup_pool, 1)
                pool.wait_ge(setup_pool, 7)
                for c in range(NC):
                    if c > 0:
                        pool.wait_ge(xc_turned, c)
                    pool.tensor_copy(xc[:, :, :], V[:, QT * c:QT * (c + 1), :]).then_inc(xc_ready, 1)
                    pool.wait_ge(xct_ready, c + 1)
                    pool.tensor_copy(XT[:, c * CHUNK:(c + 1) * CHUNK], mixed[:, :]).then_inc(xt_stored, 1)
                pool.wait_ge(xt_stored, NC)
                pool.memset(K[96:98, :, :].bitcast(F32), 1.0).then_inc(setup_pool, 1)
                for c in range(NC):
                    pool.wait_ge(variance_ready, 12 + c + 1)
                    pool.tensor_tensor(norm_rstd[:, 0:QT], norm_ve[:, 0:QT], minus_half[:, 0:QT], ALU.pow)\
                        .then_inc(rstd_ready, 1)

            @block.scalar
            def _(act):
                def keys(c):
                    act.wait_ge(xc_turned, c + 1)
                    at_least(act, values_done, c)
                    at_least(act, xt_stored, c)
                    act.activation(mixed[:, :], bank(0), ACT.Copy).then_inc(xct_ready, 1)
                    where = slice(c * CHUNK, (c + 1) * CHUNK)
                    for h in range(HEADS):
                        act.wait_ge(keys_done, HEADS * c + h + 1)
                        act.activation(K[0:96, h, where], bank(1 + h)[0:96, :], ACT.Identity,
                                       bias=bk_sb[:, h:h + 1]).then_inc(keys_hi, 1)

                for c in range(NC):
                    keys(c)

                def query(c, number, h):
                    act.wait_ge(side_done, number + 1)
                    at_least(act, queries_ready, c)
                    act.activation(QA[0:96, h, :], bank(SIDE_BANKS + h % 2)[0:96, :], ACT.Identity,
                                   bias=bq_sb[:, h:h + 1]).then_inc(query_hi, 1)

                def copy_sums(c):
                    act.wait_ge(summed, NT * (c + 1))
                    at_least(act, mixed_ready, c)
                    act.activation(denom[:, :], bank(DEN_BANK), ACT.Copy).then_inc(sums_read, 1)
                    act.activation(att[:, :], bank(OUT_BANK), ACT.Copy).then_inc(sums_read, 1)

                def gate(c, base):
                    act.wait_ge(side_read, base + 1)
                    act.activation(beta[:, :], beta[:, :], ACT.Tanh, scale=0.5).then_inc(gate_tanh, 1)
                    act.wait_ge(gate_tanh, c + 1)
                    act.activation(beta[:, :], beta[:, :], ACT.Copy, scale=0.5, bias=0.5).then_inc(gate_ready, 1)

                def copy_queries(c):
                    act.wait_ge(side_read, side_base(c))
                    at_least(act, scores_done, 2 * NT * c)
                    act.activation(QB[0:98, :, :], QA[0:98, :, :], ACT.Copy).then_inc(queries_ready, 1)

                def body(c, with_prep, with_finish):
                    for t in range(NT):
                        if t == 0 and with_prep:
                            for h in range(2):
                                query(c + 1, side_base(c) + h, h)
                        if t == 0 and with_finish:
                            copy_sums(c - 1)
                        for hp in range(2):
                            e = 2 * NT * c + 2 * t + hp
                            slot = (2 * t + hp) % 4
                            act.wait_ge(scores_done, e + 1)
                            at_least(act, summed, NT * c + t - 1)
                            act.activation(E[:, slot, :], score_banks(hp), ACT.Exp).then_inc(exp_done, 1)
                            if t == 0 and with_prep:
                                query(c + 1, side_base(c) + 2 + hp, 2 + hp)
                        if with_finish and t == GATE_AT:
                            gate(c - 1, side_base(c) + logit_at(with_prep))
                    if with_prep:
                        copy_queries(c + 1)

                for h in range(HEADS):
                    query(0, h, h)
                copy_queries(0)
                body(0, True, False)
                with act.Fori(1, NC - 1) as c:
                    body(c, True, True)
                body(NC - 1, False, True)
                copy_sums(NC - 1)
                gate(NC - 1, side_base(NC - 1) + FINISH + logit_at(False))

            @block.tensor
            def _(pe):
                pe.wait_ge(head_setup, 4)

                def keys(c):
                    pe.wait_ge(xc_ready, c + 1)
                    for t in range(QT):
                        mm = nc.tensor.transpose(bank(0)[:, t * P:(t + 1) * P], xc[:, t, :], ident[:, :])
                    mm.then_inc(xc_turned, 1)
                    pe.wait_ge(xct_ready, c + 1)
                    for h in range(HEADS):
                        at_least(pe, keys_split, HEADS * (c - 1) + h + 1)
                        nc.tensor.matmul(bank(1 + h)[0:96, :], wk_sb[:, h, :], mixed[:, :],
                                         start=True, stop=True).then_inc(keys_done, 1)
                    at_least(pe, values_ready, c)
                    for t in range(QT):
                        mm = nc.tensor.matmul(bank(5)[:, t * D:(t + 1) * D], mixed[:, t * P:(t + 1) * P],
                                              wv_sb[:, :], start=True, stop=True)
                    mm.then_inc(values_done, 1)

                for c in range(NC):
                    keys(c)

                def side(item, c, number, parity):
                    at_least(pe, side_read, number - 1)
                    dst = bank(SIDE_BANKS + parity)
                    where = slice(c * CHUNK, (c + 1) * CHUNK) if isinstance(c, int) else bass.ds(c * CHUNK, CHUNK)
                    kind = item[0]
                    if kind == "query":
                        mm = nc.tensor.matmul(dst[0:96, :], wq_sb[:, item[1], :], XT[:, where], start=True, stop=True)
                    if kind == "score":
                        _, t, h, kc = item
                        if kc == 0 and h == 0 and t == 0:
                            pe.wait_ge(side_read, number)
                        mm = nc.tensor.matmul(dst, QA[0:96, h, t * P:(t + 1) * P],
                                              K[0:96, h, kc * CHUNK:(kc + 1) * CHUNK], start=True, stop=True)
                    if kind == "maximum":
                        pe.wait_ge(spread_ready, QT * c + item[1] + 1)
                        for h in range(HEADS):
                            mm = nc.tensor.transpose(dst[0:98, h * P:(h + 1) * P], spread[:, h, :], ident[:, :])
                    if kind == "xr":
                        mm = nc.tensor.matmul(dst, ws_sb[:, :], XT[:, where], start=True, stop=True)
                    if kind == "logit":
                        pe.wait_ge(side_read, number)
                        pe.wait_ge(att_ready, c + 1)
                        nc.tensor.matmul(dst, wb_rep[:, 0, :], att[:, :], start=True, stop=False)
                        mm = nc.tensor.matmul(dst, wb_rep[:, 1, :], xr[:, :], start=False, stop=True)
                    if kind == "turn":
                        pe.wait_ge(mixed_ready, c + 1)
                        for i in range(2):
                            t = 2 * item[1] + i
                            mm = nc.tensor.transpose(dst[:, i * P:(i + 1) * P], mixed[:, t * P:(t + 1) * P],
                                                     ident[:, :])
                    mm.then_inc(side_done, 1)

                def sides(items, c, base, j):
                    for item in items:
                        chunk = c - 1 if item[0] in ("xr", "logit", "turn") else c + 1
                        side(item, chunk, base + j, j % 2)
                        j += 1
                    return j

                def scores(c, t, hp):
                    if t == 0 and hp == 0:
                        pe.wait_ge(queries_ready, c + 1)
                    if t % 2 == 0 and hp == 0:
                        pe.wait_ge(mask_t_ready, (NT // 2) * c + t // 2 + 1)
                    e = 2 * NT * c + 2 * t + hp
                    at_least(pe, exp_done, e - 1)
                    for h in (2 * hp, 2 * hp + 1):
                        nc.tensor.matmul(bank(h), ident_b[:, :], mask_t[:, (t // 2) % 2, t % 2, :],
                                         start=True, stop=False)
                        mm = nc.tensor.matmul(bank(h), K[0:98, h, t * P:(t + 1) * P], QB[0:98, h, :],
                                              start=False, stop=True)
                    mm.then_inc(scores_done, 1)

                def sum_values(c, t, dst):
                    if dst == OUT_BANK:
                        pe.wait_ge(exp_done, 2 * NT * c + 2 * t + 2)
                        if t == 0:
                            at_least(pe, sums_read, 2 * c)
                    for h in range(HEADS):
                        slot = (2 * t + h // 2) % 4
                        w = values[:, t, h * C:(h + 1) * C] if dst == OUT_BANK else ones[:, :]
                        mm = nc.tensor.matmul(bank(dst)[h * C:(h + 1) * C, :], w,
                                              E[:, slot, (h % 2) * CHUNK:(h % 2 + 1) * CHUNK],
                                              start=(t == 0), stop=(t == NT - 1))
                    if dst == DEN_BANK:
                        mm.then_inc(summed, 1)

                def body(c, with_prep, with_finish):
                    order = side_order(with_prep, with_finish)
                    j, base = 0, side_base(c)
                    for t in range(NT):
                        items = order[t]
                        if t == 0:
                            for i, dst in enumerate((OUT_BANK, DEN_BANK)):
                                if with_finish:
                                    sum_values(c - 1, NT - 1, dst)
                                j = sides(items[i:i + 1], c, base, j)
                            for hp in range(2):
                                scores(c, t, hp)
                                j = sides(items[2 + hp:3 + hp], c, base, j)
                            continue
                        scores(c, t, 0)
                        j = sides(items[0:1], c, base, j)
                        scores(c, t, 1)
                        j = sides(items[1:2], c, base, j)
                        sum_values(c, t - 1, OUT_BANK)
                        j = sides(items[2:3], c, base, j)
                        sum_values(c, t - 1, DEN_BANK)
                        j = sides(items[3:], c, base, j)

                pe.wait_ge(xt_stored, NC)
                pe.wait_ge(keys_split, HEADS * NC)
                pe.wait_ge(values_ready, NC)
                prep = [item for items in side_order(True, False) for item in items]
                sides(prep, -1, 0, 0)
                pe.wait_ge(setup_pool, 8)
                body(0, True, False)
                with pe.Fori(1, NC - 1) as c:
                    body(c, True, True)
                body(NC - 1, False, True)
                for dst in (OUT_BANK, DEN_BANK):
                    sum_values(NC - 1, NT - 1, dst)
                base = side_base(NC - 1) + FINISH
                finish = [item for items in side_order(False, True) for item in items]
                sides(finish, NC, base, 0)

            @block.vector
            def _(dve):
                chain = Chain(dve, part2_chain)
                scale = float(C) ** -0.5
                nc.vector.tensor_scalar(wq_sb[:, :, :], wq_sb[:, :, :], scale, None, ALU.mult).then_inc(head_setup, 1)
                nc.vector.tensor_scalar(bq_sb[:, :], bq_sb[:, :], scale, None, ALU.mult).then_inc(head_setup, 1)
                nc.vector.tensor_tensor(wb_rep[:, 0, :], wb_sb[:, 0:1].broadcast_to([P, P]),
                                        wb_sb[:, 2:3].broadcast_to([P, P]), ALU.add).then_inc(head_setup, 1)
                nc.vector.tensor_tensor(wb_rep[:, 1, :], wb_sb[:, 1:2].broadcast_to([P, P]),
                                        wb_sb[:, 2:3].broadcast_to([P, P]), ALU.subtract).then_inc(head_setup, 1)
                dve.wait_ge(head_setup, 4)

                def keys(c):
                    where, tiles_ = slice(c * CHUNK, (c + 1) * CHUNK), slice(QT * c, QT * (c + 1))
                    for h in range(HEADS):
                        dve.wait_ge(keys_hi, HEADS * c + h + 1)
                        nc.vector.scalar_tensor_tensor(
                            K[32:64, h, where], bank(1 + h)[32:64, :], bk_sb[32:64, h:h + 1],
                            K[32:64, h, where].bitcast(F32), op0=ALU.add, op1=ALU.subtract).then_inc(keys_split, 1)
                    dve.wait_ge(values_done, c + 1)
                    nc.vector.tensor_tensor(values[:, tiles_, :], bank(5).rearrange("p (t d) -> p t d", d=D),
                                            rows[:, RBV:RBV + 1, :].broadcast_to([P, QT, D]), ALU.add)\
                        .then_inc(values_ready, 1)

                def make_mask_t(c, j):
                    dve.wait_ge(raw_t_in[j % 2], 16 * ((NT // 4) * c + j // 2 + 1))
                    at_least(dve, scores_done, 2 * NT * c + 4 * (j - 1))
                    nc.vector.tensor_scalar(mask_t[:, j % 2, :, :], raw_t[:, j % 2, :, :], 0.0, -BIG,
                                            ALU.is_equal, ALU.mult).then_inc(mask_t_ready, 1)

                def make_mask_q(c, t, quarter):
                    dve.wait_ge(raw_q_in[quarter % 2], 16 * (2 * (QT * c + t) + quarter // 2 + 1))
                    nc.vector.tensor_scalar(mask_q[:, t % 2, quarter * 2 * CHUNK:(quarter + 1) * 2 * CHUNK],
                                            raw_q[:, quarter % 2, :], 0.0, -BIG, ALU.is_equal, ALU.mult)\
                        .then_inc(mask_q_ready, 1)

                def side(item, c, base, j):
                    number, kind = base + j, item[0]
                    dve.wait_ge(side_done, number + 1)
                    src = bank(SIDE_BANKS + j % 2)
                    if kind == "query":
                        h = item[1]
                        dve.wait_ge(query_hi, HEADS * c + h + 1)
                        nc.vector.scalar_tensor_tensor(
                            QA[64:96, h, :], src[64:96, :], bq_sb[64:96, h:h + 1], QA[64:96, h, :].bitcast(F32),
                            op0=ALU.add, op1=ALU.subtract).then_inc(side_read, 1)
                    if kind == "score":
                        _, t, h, kc = item
                        if kc % 2 == 0:
                            dve.wait_ge(mask_q_ready, 4 * (QT * c + t) + kc // 2 + 1)
                        at_least(dve, side_read, number - 3)
                        nc.vector.tensor_tensor_reduce(
                            out=masked[:, j % 4, :], in0=src,
                            in1=mask_q[:, t % 2, kc * CHUNK:(kc + 1) * CHUNK], scale=1.0, scalar=-3e38,
                            op0=ALU.add, op1=ALU.max, accum_out=maxima[:, h, kc:kc + 1]).then_inc(side_read, 1)
                        if kc == KC - 1 and QT * c + t + 1 < NT:
                            make_mask_q(*divmod(QT * c + t + 1, QT), h)
                        if kc == KC - 1 and h == HEADS - 1:
                            row_maxima(number)
                    if kind == "maximum":
                        t = item[1]
                        nc.vector.tensor_copy(QA[96:98, :, t * P:(t + 1) * P],
                                              src[96:98, :].rearrange("p (h n) -> p h n", h=HEADS))\
                            .then_inc(side_read, 1)
                    if kind == "xr":
                        nc.vector.tensor_scalar(xr[:, :], src, cols[:, BS:BS + 1], None, ALU.add)\
                            .then_inc(side_read, 1)
                    if kind == "logit":
                        nc.vector.tensor_copy(beta[:, :], src).then_inc(side_read, 1)
                    if kind == "turn":
                        if item[1] == 0:
                            at_least(dve, y_out, 16 * c)
                        for i in range(2):
                            t = 2 * item[1] + i
                            add = nc.vector.tensor_tensor(
                                y[:, t, :].rearrange("p (c h) -> p c h", h=HEADS),
                                src[:, i * P:(i + 1) * P].rearrange("p (h c) -> p c h", h=HEADS),
                                V[:, QT * c + t, :].rearrange("p (c h) -> p c h", h=HEADS), ALU.add)
                        add.then_inc(side_read, 1)
                        if item[1] == 1:
                            dve.wait_ge(side_read, number + 1)
                            norm_begin(chain, QT, y)

                def row_maxima(number):
                    dve.wait_ge(side_read, number + 1)
                    chain.link(nc.vector.tensor_reduce(row_max[:, :], maxima[:, :, :], AX.X, ALU.max))
                    chain.link(nc.vector.scalar_tensor_tensor(row_max[:, :], row_max[:, :], -BIG / 10, row_max[:, :],
                                                              op0=ALU.is_gt, op1=ALU.mult))
                    chain.link(nc.vector.tensor_scalar(minus_hi[:, :], row_max[:, :], -1.0, None, ALU.mult))
                    chain.link(nc.vector.tensor_copy(spread[:, :, 96], minus_hi[:, :].bitcast(F32)))
                    nc.vector.scalar_tensor_tensor(spread[:, :, 97], row_max[:, :], -1.0, minus_hi[:, :].bitcast(F32),
                                                   op0=ALU.mult, op1=ALU.subtract).then_inc(spread_ready, 1)

                def sides(items, c, base, j):
                    for item in items:
                        side(item, c - 1 if item[0] in ("xr", "logit", "turn") else c + 1, base, j)
                        j += 1
                    return j

                def divide(c):
                    dve.wait_ge(sums_read, 2 * c + 2)
                    chain.link(nc.vector.scalar_tensor_tensor(denom[:, :], denom[:, :], 0.0, denom[:, :],
                                                              op0=ALU.is_equal, op1=ALU.add))
                    chain.link(nc.vector.reciprocal(denom[:, :], denom[:, :]))
                    nc.vector.tensor_tensor(att[:, :], att[:, :], denom[:, :], ALU.mult).then_inc(att_ready, 1)

                def mix(c):
                    chain.link(nc.vector.tensor_tensor(xr[:, :], xr[:, :], att[:, :], ALU.subtract))
                    dve.wait_ge(gate_ready, c + 1)
                    chain.link(nc.vector.tensor_tensor(xr[:, :], xr[:, :], beta[:, :], ALU.mult))
                    nc.vector.tensor_tensor(mixed[:, :], xr[:, :], att[:, :], ALU.add).then_inc(mixed_ready, 1)

                def finish_norm(c):
                    norm_end(dve, 12 + c, QT, y, y).then_inc(y_ready, 1)

                def body(c, with_prep, with_finish):
                    order = side_order(with_prep, with_finish)
                    j, base = 0, side_base(c)
                    for t in range(NT):
                        if t % 2 == 0 and t + 2 < NT:
                            make_mask_t(c, t // 2 + 1)
                        elif t % 2 == 0 and with_prep:
                            make_mask_t(c + 1, 0)
                        if with_finish and t == DIVIDE_AT:
                            divide(c - 1)
                        if with_finish and t == MIX_AT:
                            mix(c - 1)
                        if with_finish and t == NORM_AT:
                            finish_norm(c - 1)
                        j = sides(order[t], c, base, j)

                for c in range(NC):
                    keys(c)
                for quarter in range(4):
                    make_mask_q(0, 0, quarter)
                prep = [item for items in side_order(True, False) for item in items]
                dve.wait_ge(setup_pool, 7)
                sides(prep, -1, 0, 0)
                make_mask_t(0, 0)
                for c in range(NC):
                    body(c, c < NC - 1, c > 0)
                base = side_base(NC - 1) + FINISH
                divide(NC - 1)
                sides([("xr",), ("logit",)], NC, base, 0)
                mix(NC - 1)
                sides([("turn", 0), ("turn", 1)], NC, base, 2)
                finish_norm(NC - 1)


def kernel(**inputs):
    import numpy as np
    import concourse.bacc as bacc
    from concourse import mybir as _mybir
    from concourse.bass_utils import run_bass_kernel_spmd

    a = {name: np.asarray(value) for name, value in inputs.items()}
    w_ih, w_hh = (a["L1_gnn_" + n].reshape(3, D, D) for n in ("W_ih", "W_hh"))
    b_ih, b_hh = (a["L1_gnn_" + n].reshape(3, D) for n in ("b_ih", "b_hh"))
    mats = [a["L0_gnn_" + n] for n in ("uv_W1", "uv_W2", "uv_W3", "vu_W1", "vu_W2", "vu_W3")]
    mats += [a["L1_gnn_W_msg"].T] + [w_ih[g].T for g in range(3)] + [w_hh[g].T for g in range(3)]
    mats += [a["L2_gnn_W_in"], a["L2_gnn_W_out"]]

    def by_head(columns):
        return np.swapaxes(columns.reshape(columns.shape[:-1] + (C, HEADS)), -1, -2).reshape(columns.shape)

    def thrice(w):
        return np.tile(w.reshape(D, HEADS, 1, C), (1, 1, 3, 1)).reshape(D, HEADS, 3 * C)

    cols = [a["L0_gnn_" + n] for n in ("uv_b1", "uv_b2", "vu_b1", "vu_b2")] + [a["L1_gnn_b_msg"]]
    cols += list(b_ih) + list(b_hh) + [by_head(a["L3_gnn_bs"])]
    arrays = {
        "x": a["x"],
        "adj": a["adj"],
        "adj_t": a["adj"].T,
        "weights": np.stack(mats, axis=1),
        "bias_cols": np.stack(cols, axis=1),
        "bias_rows": np.stack([a["L0_gnn_uv_b3"], a["L0_gnn_vu_b3"], a["L3_gnn_bv"]]),
        "wq_rep": thrice(a["L3_gnn_Wq"]),
        "wk_rep": thrice(a["L3_gnn_Wk"]),
        "bq_rep": np.tile(a["L3_gnn_bq"].reshape(HEADS, C).T, (3, 1)),
        "bk_rep": np.tile(a["L3_gnn_bk"].reshape(HEADS, C).T, (3, 1)),
        "wv": a["L3_gnn_Wv"],
        "ws_perm": by_head(a["L3_gnn_Ws"]),
        "wb_cols": by_head(a["L3_gnn_Wb"].reshape(3, D)).T,
    }
    nc = bacc.Bacc("TRN2", target_bir_lowering=False, num_devices=1)
    fed, args = {}, []
    for name, value in arrays.items():
        value = np.ascontiguousarray(value)
        fed[f"{name}_dram"] = value
        args.append(nc.dram_tensor(f"{name}_dram", value.shape, _mybir.dt.from_np(value.dtype),
                                   kind="ExternalInput").ap())
    out = nc.dram_tensor("out_dram", (N, D), _mybir.dt.float32, kind="ExternalOutput").ap()
    graph_kernel(nc, *args, out)
    result = run_bass_kernel_spmd(nc, [fed], core_ids=[0])
    return result.results[0]["out_dram"]
```

```python
import concourse.bass as bass
from concourse import mybir
from contextlib import ExitStack

F32 = mybir.dt.float32
F32R = mybir.dt.float32r
BF16 = mybir.dt.bfloat16
ALU = mybir.AluOpType
ACT = mybir.ActivationFunctionType
AX = mybir.AxisListType

P = 128
N = 4096
D = 128
NT = N // P
HALF = 2048
BANK = 512
NB = HALF // BANK
PAIR = 2 * BANK
PT = PAIR // P
RING = 4
X_FIRST = 4
TAIL_TILES = 16
STEPS = 6
GRU_STEPS = 9
PRODUCTS = 8
HALVES = 2 * PRODUCTS
EPS = 1e-5
SLOPE = 0.01
HEADS = 4
C = D // HEADS
CHUNK = 512
NC = N // CHUNK
QT = CHUNK // P
KC = N // CHUNK
BIG = 1e30

(UV1, UV2, UV3, VU1, VU2, VU3, WMSG, WIR, WIZ, WIN, WHR, WHZ, WHN, LIN, LOUT) = range(15)
(BUV1, BUV2, BVU1, BVU2, BMSG, BIR, BIZ, BIN, BHR, BHZ, BHN, BS) = range(12)
(RUV3, RVU3, RBV) = range(3)


def at_least(engine, semaphore, value):
    if isinstance(value, int) and value <= 0:
        return
    engine.wait_ge(semaphore, value)


class Chain:

    def __init__(self, engine, semaphore):
        self.engine, self.semaphore, self.count = engine, semaphore, 0

    def link(self, instruction):
        instruction.then_inc(self.semaphore, 1)
        self.count = self.count + 1
        self.engine.wait_ge(self.semaphore, self.count)


def graph_kernel(nc, x, adj, adj_t, weights, bias_cols, bias_rows, wq_rep, wk_rep, bq_rep, bk_rep,
                 wv, ws_perm, wb_cols, out):
    ctx = ExitStack()
    with ctx:
        def sb(name, shape, dt=F32, where=ctx):
            return where.enter_context(nc.sbuf_tensor(name, shape, dt))

        def sem(name):
            return ctx.enter_context(nc.semaphore(name))

        psum = ctx.enter_context(nc.psum_tensor("psum", [P, 8 * BANK], F32))

        V = sb("V", [P, NT, D])
        ident = sb("ident", [P, P])
        ident_b = sb("ident_b", [P, P], BF16)
        ones = sb("ones", [P, C])
        minus_half = sb("minus_half", [P, PT])
        rows = sb("rows", [P, 3, D])
        wq_sb = sb("wq_sb", [P, HEADS, 3 * C])
        wk_sb = sb("wk_sb", [P, HEADS, 3 * C])
        bq_sb = sb("bq_sb", [3 * C, HEADS])
        bk_sb = sb("bk_sb", [3 * C, HEADS])
        wv_sb = sb("wv_sb", [P, D])
        ws_sb = sb("ws_sb", [P, D])
        wb_sb = sb("wb_sb", [P, 3])
        cols = sb("cols", [P, 12])
        norm_stats = sb("norm_stats", [P, PT, 6])
        norm_mv = sb("norm_mv", [P, PT, 2])
        norm_ve = sb("norm_ve", [P, PT])
        norm_rstd = sb("norm_rstd", [P, PT])

        consts_in = sem("consts_in")
        setup_pool = sem("setup_pool")
        setup_dve = sem("setup_dve")
        dve_chain = sem("dve_chain")
        pool_chain = sem("pool_chain")
        variance_ready = sem("variance_ready")
        rstd_ready = sem("rstd_ready")

        def norm_begin(chain, count, src):
            for t in range(count):
                last = nc.vector.bn_stats(norm_stats[:, t, :], src[:, t, :])
            chain.link(last)
            for t in range(count):
                last = nc.vector.bn_aggr(norm_mv[:, t, :], norm_stats[:, t, :])
            chain.link(last)
            nc.vector.tensor_scalar(norm_ve[:, 0:count], norm_mv[:, 0:count, 1], EPS, None, ALU.add)\
                .then_inc(variance_ready, 1)

        def norm_end(dve, i, count, dst, src):
            dve.wait_ge(rstd_ready, i + 1)
            for t in range(count):
                last = nc.vector.tensor_scalar(dst[:, t, :], src[:, t, :], norm_mv[:, t, 0:1],
                                               norm_rstd[:, t:t + 1], ALU.subtract, ALU.mult)
            return last

        part = ExitStack()
        with part:
            U = sb("U", [P, NT, D], where=part)
            X0 = sb("X0", [P, NT, D], where=part)
            w_sb = sb("w_sb", [P, 15, D], where=part)
            raw = sb("raw", [P, RING, HALF], where=part)
            adj_hi = sb("adj_hi", [P, RING, HALF], F32R, where=part)
            adj_lo = sb("adj_lo", [P, RING, HALF], F32R, where=part)
            x_hi = sb("x_hi", [P, RING, D], F32R, where=part)
            x_lo = sb("x_lo", [P, RING, D], F32R, where=part)
            agg = sb("agg", [P, 2, PAIR], where=part)
            act1 = sb("act1", [P, PAIR], where=part)
            act2 = sb("act2", [P, PAIR], where=part)
            pre = sb("pre", [P, PAIR], where=part)
            gate_r = sb("gate_r", [P, PAIR], where=part)
            gate_z = sb("gate_z", [P, PAIR], where=part)
            cand = sb("cand", [P, PAIR], where=part)
            gate_bias = sb("gate_bias", [P, 2], where=part)
            col_parts = sb("col_parts", [P, 2, NT], where=part)
            row_parts = sb("row_parts", [P, 2, NT], where=part)
            inv_col_deg = sb("inv_col_deg", [P, NT], where=part)
            inv_row_deg = sb("inv_row_deg", [P, NT], where=part)
            deg_flag = sb("deg_flag", [P, NT], where=part)

            in_buf = [X0, V, U, V, U, V, U, U]
            out_buf = [V, U, V, U, V, U, X0, V]
            MLP = {0: (UV1, BUV1, RUV3), 1: (VU1, BVU1, RVU3), 2: (UV1, BUV1, RUV3),
                   3: (VU1, BVU1, RVU3), 4: (UV1, BUV1, RUV3)}
            GRU, CONV_T, CONV = 5, 6, 7
            NORMED = [4, GRU, CONV]

            x_in = sem("x_in")
            x_rest_in = sem("x_rest_in")
            raw_in = [sem(f"raw_in{s}") for s in range(RING)]
            hi_ready = sem("hi_ready")
            lo_ready = sem("lo_ready")
            stage_ready = sem("stage_ready")
            stage_hi = sem("stage_hi")
            tile_used = sem("tile_used")
            agg_ready = sem("agg_ready")
            layer1_done = sem("layer1_done")
            layer2_done = sem("layer2_done")
            layer3_done = sem("layer3_done")
            sum1_ready = sem("sum1_ready")
            sum2_ready = sem("sum2_ready")
            act1_ready = sem("act1_ready")
            act2_ready = sem("act2_ready")
            pre_ready = sem("pre_ready")
            mlp_ready = sem("mlp_ready")
            norm_ready = sem("norm_ready")
            msg_done = sem("msg_done")
            msg_ready = sem("msg_ready")
            gates_done = sem("gates_done")
            gates_tanh = sem("gates_tanh")
            gates_ready = sem("gates_ready")
            cand_done = sem("cand_done")
            cand_pre = sem("cand_pre")
            cand_ready = sem("cand_ready")
            state_ready = sem("state_ready")
            state_done = sem("state_done")
            conv_done = sem("conv_done")
            conv_ready = sem("conv_ready")

            def accumulator(half, bank):
                q = 4 * (half % 2) + bank
                return psum[:, q * BANK:(q + 1) * BANK]

            def scratch(half, which):
                q = 4 * (half % 2) + 2 * which
                return psum[:, q * BANK:(q + 2) * BANK]

            def per_tile(ap):
                return ap.rearrange("p (t d) -> p t d", d=D)

            def pair_of(buf, half, k):
                t0 = (half % 2) * (HALF // P) + k * PT
                return buf[:, t0:t0 + PT, :]

            def whole(product):
                return product in (GRU, CONV_T)

            def tail_steps(tail, h, hs, n):
                if hs > 0:
                    last = (hs - 1) // 2
                    for k in range(2):
                        tail(h, hs - 1, last, k, n - k * (GRU_STEPS if last == GRU else STEPS))

            def halves(engine, half_body, constants):
                half_body(0, 0)
                constants()
                with engine.Fori(0, 2) as r:
                    for hs in range(1, 5):
                        half_body(hs + 4 * r, hs)
                for h in range(9, HALVES):
                    half_body(h, h)

            def tiles(engine, hs, tile_body, tail_body):
                for n in range(TAIL_TILES):
                    tile_body(n, n, n // RING)
                    tail_body(n)
                if whole(hs // 2):
                    for n in range(TAIL_TILES, NT):
                        tile_body(n, n, n // RING)
                        tail_body(n)
                else:
                    with engine.Fori(TAIL_TILES // RING, NT // RING - 1) as g:
                        for s in range(RING):
                            tile_body(RING * g + s, TAIL_TILES + s, g)
                    for n in range(NT - RING, NT):
                        tile_body(n, n, n // RING)

            with nc.Block() as block:

                @block.sync
                def _(sp):
                    x_tiles = x.rearrange("(t p) d -> p t d", p=P)
                    sp.dma_start(X0[:, 0:X_FIRST, :], x_tiles[:, 0:X_FIRST, :]).then_inc(x_in, 16)

                    def half_body(h, hs):
                        source = adj if hs // 2 == CONV_T else adj_t
                        c0 = (hs % 2) * HALF

                        def load(n, s, g):
                            at_least(sp, lo_ready, NT * h + n - RING + 1)
                            if isinstance(n, int):
                                src = source[n * P:(n + 1) * P, c0:c0 + HALF]
                            else:
                                src = source[bass.ds(n * P, P), c0:c0 + HALF]
                            sp.dma_start(raw[:, s % RING, :], src).then_inc(raw_in[s % RING], 16)

                        def rest_of_x(n):
                            if hs == 0 and n == 1:
                                sp.dma_start(X0[:, X_FIRST:NT, :], x_tiles[:, X_FIRST:NT, :])\
                                    .then_inc(x_rest_in, 16)

                        tiles(sp, hs, load, rest_of_x)

                    halves(sp, half_body, lambda: None)

                @block.gpsimd
                def _(pool):
                    pool.memset(ident[:, :], 0.0).then_inc(setup_pool, 1)
                    pool.memset(ident_b[:, :], 0.0).then_inc(setup_pool, 1)
                    pool.memset(ones[:, :], 1.0).then_inc(setup_pool, 1)
                    pool.memset(minus_half[:, :], -0.5).then_inc(setup_pool, 1)
                    pool.wait_ge(setup_pool, 4)
                    for m in (ident, ident_b):
                        pool.affine_select(out=m[:, :], in_=m[:, :], compare_op=ALU.not_equal, fill=1.0,
                                           base=0, pattern=[[-1, P]], channel_multiplier=1)\
                            .then_inc(setup_pool, 1)
                    pool.wait_ge(x_in, 16)
                    pool.wait_ge(setup_pool, 6)

                    def stage(h, n):
                        product, first_half = h // 2, h % 2 == 0
                        source = in_buf[product]
                        if first_half and product > 0 and n % PT == 0:
                            pairs = 2 * (n // PT + 1)
                            if product < GRU:
                                pool.wait_ge(mlp_ready, 4 * (h - 2) + pairs)
                            elif product == GRU:
                                pool.wait_ge(norm_ready, pairs)
                            elif product == CONV_T:
                                pool.wait_ge(norm_ready, 8 + pairs)
                        if h == 0 and n == X_FIRST:
                            pool.wait_ge(x_rest_in, 16)
                        at_least(pool, tile_used, NT * h + n + 2 - RING)
                        slots = slice(n % RING, n % RING + 2)
                        pool.tensor_copy(x_hi[:, slots, :], source[:, n:n + 2, :]).then_inc(stage_hi, 1)
                        pool.wait_ge(stage_hi, (NT * h + n) // 2 + 1)
                        pool.tensor_tensor(x_lo[:, slots, :], source[:, n:n + 2, :],
                                           x_hi[:, slots, :].bitcast(F32), ALU.subtract)\
                            .then_inc(stage_ready, 2)

                    def rsqrt(i):
                        pool.wait_ge(variance_ready, i + 1)
                        pool.tensor_tensor(norm_rstd[:, :], norm_ve[:, :], minus_half[:, :], ALU.pow)\
                            .then_inc(rstd_ready, 1)

                    for h in range(HALVES):
                        for n in range(0, NT, 2):
                            stage(h, n)
                            last = (h - 1) // 2
                            at = {4: (8, 14), GRU: (10, 20), CONV: (4, 10)}.get(last)
                            if last in NORMED and n in at:
                                rsqrt(4 * NORMED.index(last) + 2 * ((h - 1) % 2) + at.index(n))
                    for k in range(2):
                        rsqrt(4 * NORMED.index(CONV) + 2 + k)

                @block.scalar
                def _(act):
                    def load_constants():
                        act.dma_start(w_sb[:, :, :], weights).then_inc(consts_in, 16)
                        act.dma_start(cols[:, :], bias_cols).then_inc(consts_in, 16)
                        for r in range(3):
                            act.dma_start(rows[:, r, :], bias_rows[r].partition_broadcast(P)).then_inc(consts_in, 16)
                        for dst, src in ((wq_sb[:, :, :], wq_rep), (wk_sb[:, :, :], wk_rep), (bq_sb[:, :], bq_rep),
                                         (bk_sb[:, :], bk_rep), (wv_sb[:, :], wv), (ws_sb[:, :], ws_perm),
                                         (wb_sb[:, :], wb_cols)):
                            act.dma_start(dst, src).then_inc(consts_in, 16)

                    def half_body(h, hs):
                        product = hs // 2

                        def make_hi(n, s, g):
                            slot = s % RING
                            act.wait_ge(raw_in[slot], 16 * ((NT // RING) * h + g + 1))
                            at_least(act, tile_used, NT * h + n - RING + 1)
                            sums = {}
                            if whole(product):
                                parts = col_parts if product == GRU else row_parts
                                sums = dict(accum_out=parts[:, hs % 2, n:n + 1])
                            act.activation(adj_hi[:, slot, :], raw[:, slot, :], ACT.Copy, **sums)\
                                .then_inc(hi_ready, 1)

                        def after(n):
                            if hs == 0 and n == RING:
                                load_constants()
                            if hs > 0 and n in (3, 4):
                                act.wait_ge(tile_used, NT * h)
                                act.activation(agg[:, n - 3, :], scratch(hs - 1, n - 3), ACT.Copy)\
                                    .then_inc(agg_ready, 1)
                            tail_steps(tail, h, hs, n)

                        tiles(act, hs, make_hi, after)

                    def tail(h, before, last, k, step):
                        pair = 2 * (h - 1) + k
                        if last <= 4:
                            b1 = MLP[last][1]
                            if step == 4:
                                act.wait_ge(layer1_done, pair + 1)
                                act.activation(act1[:, :], scratch(before, k), ACT.Identity,
                                               bias=cols[:, b1:b1 + 1]).then_inc(sum1_ready, 1)
                            if step == 6:
                                act.wait_ge(layer2_done, pair + 1)
                                act.activation(act2[:, :], scratch(before, k), ACT.Identity,
                                               bias=cols[:, b1 + 1:b1 + 2]).then_inc(sum2_ready, 1)
                        if last == GRU:
                            i = pair - 4 * GRU
                            if step == 4:
                                act.wait_ge(msg_done, i + 1)
                                act.activation(act1[:, :], scratch(before, 0), ACT.Relu,
                                               bias=cols[:, BMSG:BMSG + 1]).then_inc(msg_ready, 1)
                                act.activation(act2[:, :], scratch(before, 1), ACT.Copy).then_inc(msg_ready, 1)
                            for j, gate in enumerate((gate_r, gate_z)):
                                if step == 6 + j:
                                    act.wait_ge(gates_done, 2 * i + j + 1)
                                    act.activation(gate[:, :], scratch(before, j), ACT.Tanh, scale=0.5,
                                                   bias=gate_bias[:, j:j + 1]).then_inc(gates_tanh, 1)
                                    act.wait_ge(gates_tanh, 2 * i + j + 1)
                                    act.activation(gate[:, :], gate[:, :], ACT.Copy, scale=0.5, bias=0.5)\
                                        .then_inc(gates_ready, 1)
                            if step == 9:
                                act.wait_ge(cand_pre, i + 1)
                                act.activation(cand[:, :], pre[:, :], ACT.Tanh).then_inc(cand_ready, 1)

                    def constants():
                        act.wait_ge(consts_in, 16 * 12)
                        act.wait_ge(setup_dve, 2)

                    halves(act, half_body, constants)
                    for k in range(2):
                        act.wait_ge(tile_used, NT * HALVES)
                        act.activation(agg[:, k, :], scratch(HALVES - 1, k), ACT.Copy).then_inc(agg_ready, 1)
                    for n in range(TAIL_TILES):
                        tail_steps(tail, HALVES, HALVES, n)

                @block.tensor
                def _(pe):

                    def half_body(h, hs):
                        def multiply(n, s, g):
                            slot = s % RING
                            at = NT * h + n
                            first, final = s == 0, s == NT - 1
                            if first and hs >= 2:
                                done = (hs - 2) // 2
                                if done <= 4:
                                    pe.wait_ge(pre_ready, 2 * (h - 1))
                                elif done == GRU:
                                    pe.wait_ge(norm_ready, 2 * 2 * (h - 1) - 2 * 4 * 4)
                                else:
                                    pe.wait_ge(conv_ready, 2 * (h - 1) - 4 * CONV_T)
                            if s % 2 == 0:
                                pe.wait_ge(stage_ready, at + 2)
                            pe.wait_ge(hi_ready, at + 1)
                            for b in range(NB):
                                nc.tensor.matmul(accumulator(hs, b), x_hi[:, slot, :],
                                                 adj_hi[:, slot, b * BANK:(b + 1) * BANK], start=first, stop=False)
                            for b in range(NB):
                                nc.tensor.matmul(accumulator(hs, b), x_lo[:, slot, :],
                                                 adj_hi[:, slot, b * BANK:(b + 1) * BANK], start=False, stop=False)
                            pe.wait_ge(lo_ready, at + 1)
                            for b in range(NB):
                                mm = nc.tensor.matmul(accumulator(hs, b), x_hi[:, slot, :],
                                                      adj_lo[:, slot, b * BANK:(b + 1) * BANK],
                                                      start=False, stop=final)
                            mm.then_inc(tile_used, 1)

                        tiles(pe, hs, multiply, lambda n: tail_steps(tail, h, hs, n))

                    def dense(out_, w, rhs, start=True, stop=True):
                        for b in range(2):
                            mm = nc.tensor.matmul(out_[:, b * BANK:(b + 1) * BANK], w_sb[:, w, :],
                                                  rhs[:, b * BANK:(b + 1) * BANK], start=start, stop=stop)
                        return mm

                    def dense_to_rows(out_, lhs, w):
                        for t in range(PT):
                            mm = nc.tensor.matmul(out_[:, t * D:(t + 1) * D], lhs[:, t * P:(t + 1) * P],
                                                  w_sb[:, w, :], start=True, stop=True)
                        return mm

                    def tail(h, before, last, k, step):
                        pair = 2 * (h - 1) + k
                        if last <= 4:
                            w1 = MLP[last][0]
                            if step == 1:
                                pe.wait_ge(agg_ready, pair + 1)
                                dense(scratch(before, k), w1, agg[:, k, :]).then_inc(layer1_done, 1)
                            if step == 3:
                                pe.wait_ge(act1_ready, pair + 1)
                                dense(scratch(before, k), w1 + 1, act1[:, :]).then_inc(layer2_done, 1)
                            if step == 5:
                                pe.wait_ge(act2_ready, pair + 1)
                                dense_to_rows(scratch(before, k), act2[:, :], w1 + 2).then_inc(layer3_done, 1)
                        if last == GRU:
                            i = pair - 4 * GRU
                            if step == 2:
                                pe.wait_ge(agg_ready, 2 * h)
                                if k == 1:
                                    pe.wait_ge(norm_ready, 8 + 2 * i)
                                dense(scratch(before, 0), WMSG, agg[:, k, :])
                                old = pair_of(in_buf[last], before, k)
                                for t in range(PT):
                                    mm = nc.tensor.transpose(scratch(before, 1)[:, t * P:(t + 1) * P],
                                                             old[:, t, :], ident[:, :])
                                mm.then_inc(msg_done, 1)
                            if step in (4, 5):
                                pe.wait_ge(msg_ready, 2 * i + 2)
                                wi, wh = ((WIR, WHR), (WIZ, WHZ))[step - 4]
                                dense(scratch(before, step - 4), wi, act1[:, :], stop=False)
                                dense(scratch(before, step - 4), wh, act2[:, :], start=False)\
                                    .then_inc(gates_done, 1)
                            if step == 7:
                                pe.wait_ge(gates_tanh, 2 * i + 2)
                                dense(scratch(before, 0), WHN, act2[:, :])
                                dense(scratch(before, 1), WIN, act1[:, :]).then_inc(cand_done, 1)
                            if step == 9:
                                pe.wait_ge(state_ready, i + 1)
                                for t in range(PT):
                                    mm = nc.tensor.transpose(scratch(before, 0)[:, t * D:(t + 1) * D],
                                                             gate_z[:, t * P:(t + 1) * P], ident[:, :])
                                mm.then_inc(state_done, 1)
                        if last in (CONV_T, CONV) and step == 1:
                            pe.wait_ge(agg_ready, pair + 1)
                            dense_to_rows(scratch(before, k), agg[:, k, :],
                                          LOUT if last == CONV_T else LIN).then_inc(conv_done, 1)

                    def constants():
                        pe.wait_ge(consts_in, 16 * 12)
                        pe.wait_ge(setup_pool, 6)

                    halves(pe, half_body, constants)
                    for n in range(TAIL_TILES):
                        tail_steps(tail, HALVES, HALVES, n)

                @block.vector
                def _(dve):
                    chain = Chain(dve, dve_chain)

                    def constants():
                        dve.wait_ge(consts_in, 16 * 12)
                        for g, (bi, bh) in enumerate(((BIR, BHR), (BIZ, BHZ))):
                            chain.link(nc.vector.tensor_tensor(gate_bias[:, g:g + 1], cols[:, bi:bi + 1],
                                                               cols[:, bh:bh + 1], ALU.add))
                            nc.vector.tensor_scalar(gate_bias[:, g:g + 1], gate_bias[:, g:g + 1], 0.5, None,
                                                    ALU.mult).then_inc(setup_dve, 1)

                    def half_body(h, hs):
                        def make_lo(n, s, g):
                            slot = s % RING
                            dve.wait_ge(hi_ready, NT * h + n + 1)
                            nc.vector.tensor_tensor(adj_lo[:, slot, :], raw[:, slot, :],
                                                    adj_hi[:, slot, :].bitcast(F32), ALU.subtract)\
                                .then_inc(lo_ready, 1)

                        def after(n):
                            if n == 1 and hs in (2 * CONV_T, 2 * CONV):
                                degrees(*((col_parts, inv_col_deg) if hs == 2 * CONV_T
                                          else (row_parts, inv_row_deg)))
                            tail_steps(tail, h, hs, n)

                        tiles(dve, hs, make_lo, after)

                    def leaky(dst, src):
                        return nc.vector.scalar_tensor_tensor(dst, src, SLOPE, src, op0=ALU.mult, op1=ALU.max)

                    def degrees(parts, inverse):
                        chain.link(nc.vector.tensor_tensor(inverse[:, :], parts[:, 0, :], parts[:, 1, :], ALU.add))
                        chain.link(nc.vector.tensor_scalar(deg_flag[:, :], inverse[:, :], 0.0, None, ALU.is_gt))
                        chain.link(nc.vector.tensor_tensor(inverse[:, :], inverse[:, :], deg_flag[:, :], ALU.mult))
                        chain.link(nc.vector.tensor_scalar(deg_flag[:, :], deg_flag[:, :], -1.0, 1.0,
                                                           ALU.mult, ALU.add))
                        chain.link(nc.vector.tensor_tensor(inverse[:, :], inverse[:, :], deg_flag[:, :], ALU.add))
                        chain.link(nc.vector.reciprocal(inverse[:, :], inverse[:, :]))

                    def tail(h, before, last, k, step):
                        pair = 2 * (h - 1) + k
                        if last < GRU and step == 4:
                            dve.wait_ge(sum1_ready, pair + 1)
                            leaky(act1[:, :], act1[:, :]).then_inc(act1_ready, 1)
                        if last < GRU and step == 6:
                            dve.wait_ge(sum2_ready, pair + 1)
                            leaky(act2[:, :], act2[:, :]).then_inc(act2_ready, 1)
                        if last < GRU and step == 8:
                            dve.wait_ge(layer3_done, pair + 1)
                            r3 = MLP[last][2]
                            nc.vector.tensor_tensor(
                                per_tile(pre[:, :]), per_tile(scratch(before, k)),
                                rows[:, r3:r3 + 1, :].broadcast_to([P, PT, D]), ALU.add).then_inc(pre_ready, 1)
                            dve.wait_ge(pre_ready, pair + 1)
                            dst = pair_of(out_buf[last], before, k) if last < 4 else per_tile(cand[:, :])
                            leaky(dst, per_tile(pre[:, :])).then_inc(mlp_ready, 2)
                        if last == 4 and step == 8:
                            dve.wait_ge(mlp_ready, 2 * pair + 2)
                            chain.link(nc.vector.tensor_tensor(per_tile(cand[:, :]), per_tile(cand[:, :]),
                                                               pair_of(X0, before, k), ALU.add))
                            norm_begin(chain, PT, per_tile(cand[:, :]))
                        if last == 4 and step == 9:
                            norm_end(dve, pair - 16, PT, pair_of(out_buf[last], before, k),
                                     per_tile(cand[:, :])).then_inc(norm_ready, 2)
                        if last == GRU:
                            i = pair - 4 * GRU
                            if step == 9:
                                dve.wait_ge(cand_done, i + 1)
                                dve.wait_ge(gates_ready, 2 * i + 2)
                                chain.link(nc.vector.scalar_tensor_tensor(
                                    pre[:, :], scratch(before, 0), cols[:, BHN:BHN + 1], gate_r[:, :],
                                    op0=ALU.add, op1=ALU.mult))
                                nc.vector.scalar_tensor_tensor(
                                    pre[:, :], scratch(before, 1), cols[:, BIN:BIN + 1], pre[:, :],
                                    op0=ALU.add, op1=ALU.add).then_inc(cand_pre, 1)
                            if step == 10:
                                dve.wait_ge(cand_ready, i + 1)
                                chain.link(nc.vector.tensor_tensor(act2[:, :], act2[:, :], cand[:, :], ALU.subtract))
                                chain.link(nc.vector.tensor_tensor(act2[:, :], act2[:, :], gate_z[:, :], ALU.mult))
                                nc.vector.tensor_tensor(gate_z[:, :], act2[:, :], cand[:, :], ALU.add)\
                                    .then_inc(state_ready, 1)
                            if step == 11:
                                dve.wait_ge(state_done, i + 1)
                                old = pair_of(in_buf[last], before, k)
                                chain.link(nc.vector.tensor_tensor(per_tile(pre[:, :]), per_tile(scratch(before, 0)),
                                                                   old, ALU.add))
                                norm_begin(chain, PT, per_tile(pre[:, :]))
                            if step == 12:
                                norm_end(dve, 4 + i, PT, pair_of(out_buf[last], before, k),
                                         per_tile(pre[:, :])).then_inc(norm_ready, 2)
                        if last in (CONV_T, CONV) and step == 4:
                            i = pair - 4 * CONV_T
                            dve.wait_ge(conv_done, i + 1)
                            t0 = (before % 2) * (HALF // P) + k * PT
                            inverse = inv_col_deg if last == CONV_T else inv_row_deg
                            dst = pair_of(X0, before, k) if last == CONV_T else per_tile(pre[:, :])
                            if last == CONV:
                                dve.wait_ge(norm_ready, 16 + 2 * (i - 4))
                            nc.vector.tensor_tensor(
                                dst, per_tile(scratch(before, k)),
                                inverse[:, t0:t0 + PT].rearrange("p (t o) -> p t o", o=1).broadcast_to([P, PT, D]),
                                ALU.mult).then_inc(conv_ready, 1)
                            if last == CONV:
                                dve.wait_ge(conv_ready, i + 1)
                                for other in (X0, U):
                                    chain.link(nc.vector.tensor_tensor(
                                        per_tile(pre[:, :]), per_tile(pre[:, :]), pair_of(other, before, k), ALU.add))
                                norm_begin(chain, PT, per_tile(pre[:, :]))
                        if last == CONV and step == 5:
                            norm_end(dve, 4 + pair - 4 * CONV_T, PT, pair_of(V, before, k),
                                     per_tile(pre[:, :])).then_inc(norm_ready, 2)

                    halves(dve, half_body, constants)
                    for n in range(TAIL_TILES):
                        tail_steps(tail, HALVES, HALVES, n)

        K = sb("K", [P, HEADS, N], F32R)
        QA = sb("QA", [P, HEADS, CHUNK], F32R)
        QB = sb("QB", [P, HEADS, CHUNK], F32R)
        values = sb("values", [P, NT, D])
        raw_t = sb("raw_t", [P, 2, 2, CHUNK])
        mask_t = sb("mask_t", [P, 2, 2, CHUNK], BF16)
        raw_q = sb("raw_q", [P, 2, 2 * CHUNK])
        mask_q = sb("mask_q", [P, 2, N], BF16)
        masked = sb("masked", [P, 4, CHUNK], BF16)
        maxima = sb("maxima", [P, HEADS, KC])
        row_max = sb("row_max", [P, HEADS])
        minus_hi = sb("minus_hi", [P, HEADS], F32R)
        spread = sb("spread", [P, HEADS, 98])
        E = sb("E", [P, 3, HEADS * CHUNK])
        wb_rep = sb("wb_rep", [P, 2, P])
        xc = sb("xc", [P, QT, D])
        denom = sb("denom", [P, CHUNK])
        att = sb("att", [P, CHUNK])
        xt = sb("xt", [P, CHUNK])
        xr = sb("xr", [P, CHUNK])
        xr_next = sb("xr_next", [P, CHUNK])
        beta = sb("beta", [P, CHUNK])
        mixed = sb("mixed", [P, CHUNK])
        y = sb("y", [P, QT, D])

        xc_ready = sem("xc_ready")
        xc_turned = sem("xc_turned")
        xct_ready = sem("xct_ready")
        keys_done = sem("keys_done")
        keys_hi = sem("keys_hi")
        keys_split = sem("keys_split")
        values_done = sem("values_done")
        values_ready = sem("values_ready")
        head_setup = sem("head_setup")
        raw_t_in = [sem(f"raw_t_in{s}") for s in range(2)]
        raw_q_in = [sem(f"raw_q_in{s}") for s in range(2)]
        mask_t_ready = sem("mask_t_ready")
        mask_q_ready = sem("mask_q_ready")
        side_done = sem("side_done")
        side_read = sem("side_read")
        spread_ready = sem("spread_ready")
        queries_ready = sem("queries_ready")
        scores_done = sem("scores_done")
        exp_done = sem("exp_done")
        summed = sem("summed")
        pair_added = sem("pair_added")
        counted = sem("counted")
        sums_read = sem("sums_read")
        denoms_read = sem("denoms_read")
        att_ready = sem("att_ready")
        part2_chain = sem("part2_chain")
        query_hi = sem("query_hi")
        gate_tanh = sem("gate_tanh")
        gate_ready = sem("gate_ready")
        mixed_ready = sem("mixed_ready")
        y_ready = sem("y_ready")
        y_out = sem("y_out")

        PAIRS = NT // 2
        PREP = HEADS + QT * (HEADS * KC + 1) + 2
        FINISH = 2

        DIVIDE_AT, LOGIT_AT, GATE_AT, MIX_AT, XR_AT, TURN_AT, NORM_AT = 3, 8, 9, 11, 12, 14, 16

        def bank(b):
            return psum[:, b * BANK:(b + 1) * BANK]

        OUT_BANK, DEN_BANK = 2, 3
        SIDE_BANKS, SIDES = 4, 4
        assert (PREP - FINISH) % SIDES == 0 and (PREP + FINISH) % SIDES == 0

        def side_bank(c, j):
            first = {0: PREP, NC: FINISH}.get(c, 0) if isinstance(c, int) else 0
            return bank(SIDE_BANKS + (first + j) % SIDES)

        def side_order(with_prep, with_finish):
            order = [[] for _ in range(NT)]
            if with_prep:
                order[0] += [("x",)] + [("query", h) for h in range(HEADS)]
                order[XR_AT] += [("xr",)]
            if with_finish:
                order[LOGIT_AT] += [("logit",)]
                order[TURN_AT] += [("turn",)]
            if with_prep:
                rest = []
                for t in range(QT):
                    for u, (h, kc) in enumerate((h, kc) for h in range(HEADS) for kc in range(KC)):
                        rest.append(("score", t, h, kc))
                        if t > 0 and u == 7:
                            rest.append(("maximum", t - 1))
                t = 1
                while rest:
                    busy = {1: 2, DIVIDE_AT: 2, LOGIT_AT: 1, MIX_AT: 2, XR_AT: 1, TURN_AT: 2, NORM_AT: 1}
                    count = (4 if t % 2 == 0 else 6) - busy.get(t, 0)
                    order[t] += rest[:count]
                    rest, t = rest[count:], t + 1
                assert t < NT
                order[t] += [("maximum", QT - 1)]
            return order

        def side_base(c):
            if isinstance(c, int) and c == 0:
                return PREP
            return (PREP - FINISH) + (PREP + FINISH) * c

        def exp_slot(t):
            return (t // 2) % 2 if t % 2 == 0 else 2

        def logit_at(with_prep):
            return [item for items in side_order(with_prep, True) for item in items].index(("logit",))

        with nc.Block() as block:

            @block.sync
            def _(sp):
                def load_t(c, j):
                    at_least(sp, mask_t_ready, (NT // 2) * c + j - 1)
                    cols_ = slice(c * CHUNK, (c + 1) * CHUNK) if isinstance(c, int) else bass.ds(c * CHUNK, CHUNK)
                    src = adj_t.rearrange("(t p) n -> p t n", p=P)[:, 2 * j:2 * j + 2, cols_]
                    sp.dma_start(raw_t[:, j % 2, :, :], src).then_inc(raw_t_in[j % 2], 16)

                def load_q(c, t, quarter):
                    at_least(sp, mask_q_ready, 4 * (QT * c + t) + quarter - 1)
                    row = (QT * c + t) * P
                    rows_ = slice(row, row + P) if isinstance(c, int) else bass.ds(row, P)
                    sp.dma_start(raw_q[:, quarter % 2, :], adj[rows_, quarter * 2 * CHUNK:(quarter + 1) * 2 * CHUNK])\
                        .then_inc(raw_q_in[quarter % 2], 16)

                def body(c, with_prep, with_finish, more=True):
                    order = side_order(with_prep, with_finish)
                    for t in range(NT):
                        if t % 2 == 0 and t + 2 < NT:
                            load_t(c, t // 2 + 1)
                        elif t % 2 == 0 and with_prep:
                            load_t(c + 1, 0)
                        for item in order[t]:
                            if item[0] == "score" and item[3] == KC - 1:
                                if item[1] + 1 < QT:
                                    load_q(c + 1, item[1] + 1, item[2])
                                elif more:
                                    load_q(c + 2, 0, item[2])
                        if with_finish and t == 16:
                            store(c - 1)

                def store(c):
                    rows_ = slice(c * CHUNK, (c + 1) * CHUNK) if isinstance(c, int) else bass.ds(c * CHUNK, CHUNK)
                    sp.wait_ge(y_ready, c + 1)
                    sp.dma_start(out[rows_, :].rearrange("(t p) d -> p t d", p=P), y[:, :, :]).then_inc(y_out, 16)

                for t in range(QT):
                    for quarter in range(4):
                        load_q(0, t, quarter)
                for quarter in range(4):
                    load_q(1, 0, quarter)
                load_t(0, 0)
                body(0, True, False)
                with sp.Fori(1, NC - 2) as c:
                    body(c, True, True)
                body(NC - 2, True, True, more=False)
                body(NC - 1, False, True)
                store(NC - 1)
                sp.wait_ge(y_out, 16 * NC)

            @block.gpsimd
            def _(pool):
                pool.memset(spread[:, :, :], 0.0).then_inc(setup_pool, 1)
                pool.wait_ge(setup_pool, 7)

                def stage_x(c):
                    pool.tensor_copy(xc[:, :, :], V[:, QT * c:QT * (c + 1), :]).then_inc(xc_ready, 1)

                def rsqrt(c):
                    pool.wait_ge(variance_ready, 12 + c + 1)
                    pool.tensor_tensor(norm_rstd[:, 0:QT], norm_ve[:, 0:QT], minus_half[:, 0:QT], ALU.pow)\
                        .then_inc(rstd_ready, 1)

                for c in range(NC):
                    if c > 0:
                        pool.wait_ge(xc_turned, c)
                    stage_x(c)
                pool.wait_ge(xc_turned, NC)
                pool.memset(K[96:98, :, :].bitcast(F32), 1.0).then_inc(setup_pool, 1)
                pool.wait_ge(setup_pool, 8)
                stage_x(0)
                pool.wait_ge(side_done, 1)
                stage_x(1)
                for c in range(NC):
                    for q in range(PAIRS):
                        if q == 1 and c + 2 < NC:
                            pool.wait_ge(side_done, side_base(c) + 1)
                            stage_x(c + 2)
                        for hp in range(2):
                            part_ = slice(2 * hp * CHUNK, 2 * (hp + 1) * CHUNK)
                            pool.wait_ge(exp_done, HEADS * (NT * c + 2 * q + 1) + 2 * hp + 2)
                            pool.wait_ge(summed, NT * c + 2 * q + 1)
                            pool.tensor_tensor(E[:, q % 2, part_], E[:, q % 2, part_], E[:, 2, part_], ALU.add)\
                                .then_inc(pair_added, 1)
                        if c > 0 and 2 * q == TURN_AT:
                            rsqrt(c - 1)
                rsqrt(NC - 1)

            @block.scalar
            def _(act):
                def keys(c):
                    act.wait_ge(xc_turned, c + 1)
                    at_least(act, values_done, c)
                    act.activation(xt[:, :], bank(0), ACT.Copy).then_inc(xct_ready, 1)
                    where = slice(c * CHUNK, (c + 1) * CHUNK)
                    for h in range(HEADS):
                        act.wait_ge(keys_done, HEADS * c + h + 1)
                        act.activation(K[0:96, h, where], bank(1 + h)[0:96, :], ACT.Identity,
                                       bias=bk_sb[:, h:h + 1]).then_inc(keys_hi, 1)

                for c in range(NC):
                    keys(c)

                def query(c, number, h):
                    act.wait_ge(side_done, number + 1)
                    at_least(act, queries_ready, c)
                    act.activation(QA[0:96, h, :], side_bank(c - 1, 1 + h)[0:96, :], ACT.Identity,
                                   bias=bq_sb[:, h:h + 1]).then_inc(query_hi, 1)

                def copy_sums(c):
                    act.wait_ge(summed, NT * (c + 1))
                    at_least(act, mixed_ready, c)
                    act.activation(att[:, :], bank(OUT_BANK), ACT.Copy).then_inc(sums_read, 1)

                def copy_denominators(c):
                    act.wait_ge(counted, PAIRS * (c + 1))
                    act.activation(denom[:, :], bank(DEN_BANK), ACT.Copy).then_inc(denoms_read, 1)

                def gate(c, base):
                    act.wait_ge(side_read, base + 1)
                    act.activation(beta[:, :], beta[:, :], ACT.Tanh, scale=0.5).then_inc(gate_tanh, 1)
                    act.wait_ge(gate_tanh, c + 1)
                    act.activation(beta[:, :], beta[:, :], ACT.Copy, scale=0.5, bias=0.5).then_inc(gate_ready, 1)

                def copy_queries(c):
                    act.wait_ge(side_read, side_base(c))
                    at_least(act, scores_done, HEADS * NT * c)
                    act.activation(QB[0:98, :, :], QA[0:98, :, :], ACT.Copy).then_inc(queries_ready, 1)

                def body(c, with_prep, with_finish):
                    for t in range(NT):
                        if t == 0 and with_prep:
                            query(c + 1, side_base(c) + 1, 0)
                        if t == 0 and with_finish:
                            copy_sums(c - 1)
                        if t == 2 and with_finish:
                            copy_denominators(c - 1)
                        for h in range(HEADS):
                            act.wait_ge(scores_done, HEADS * (NT * c + t) + h + 1)
                            q = t // 2
                            if t % 2 == 0 and h == 0:
                                at_least(act, counted, PAIRS * c + q - 1)
                            if t % 2 == 1 and h == 0:
                                at_least(act, summed, NT * c + t - 1)
                            if t % 2 == 1 and h % 2 == 0:
                                at_least(act, pair_added, 2 * (PAIRS * c + q - 1) + h // 2 + 1)
                            act.activation(E[:, exp_slot(t), h * CHUNK:(h + 1) * CHUNK], bank(h % 2), ACT.Exp)\
                                .then_inc(exp_done, 1)
                            if t == 0 and with_prep and h > 0:
                                query(c + 1, side_base(c) + 1 + h, h)
                        if with_finish and t == GATE_AT:
                            gate(c - 1, side_base(c) + logit_at(with_prep))
                    if with_prep:
                        copy_queries(c + 1)

                for h in range(HEADS):
                    query(0, 1 + h, h)
                copy_queries(0)
                body(0, True, False)
                with act.Fori(1, NC - 1) as c:
                    body(c, True, True)
                body(NC - 1, False, True)
                copy_sums(NC - 1)
                copy_denominators(NC - 1)
                gate(NC - 1, side_base(NC - 1) + FINISH + logit_at(False))

            @block.tensor
            def _(pe):
                pe.wait_ge(head_setup, 4)

                def keys(c):
                    pe.wait_ge(xc_ready, c + 1)
                    for t in range(QT):
                        mm = nc.tensor.transpose(bank(0)[:, t * P:(t + 1) * P], xc[:, t, :], ident[:, :])
                    mm.then_inc(xc_turned, 1)
                    pe.wait_ge(xct_ready, c + 1)
                    for h in range(HEADS):
                        at_least(pe, keys_split, HEADS * (c - 1) + h + 1)
                        nc.tensor.matmul(bank(1 + h)[0:96, :], wk_sb[:, h, :], xt[:, :],
                                         start=True, stop=True).then_inc(keys_done, 1)
                    at_least(pe, values_ready, c)
                    for t in range(QT):
                        mm = nc.tensor.matmul(bank(5)[:, t * D:(t + 1) * D], xt[:, t * P:(t + 1) * P],
                                              wv_sb[:, :], start=True, stop=True)
                    mm.then_inc(values_done, 1)

                for c in range(NC):
                    keys(c)

                def side(item, c, number, dst):
                    at_least(pe, side_read, number + 1 - SIDES)
                    kind = item[0]
                    if kind == "x":
                        pe.wait_ge(xc_ready, NC + c + 1)
                        for t in range(QT):
                            mm = nc.tensor.transpose(dst[:, t * P:(t + 1) * P], xc[:, t, :], ident[:, :])
                    if kind == "query":
                        if item[1] == 0:
                            pe.wait_ge(side_read, number)
                        mm = nc.tensor.matmul(dst[0:96, :], wq_sb[:, item[1], :], xt[:, :], start=True, stop=True)
                    if kind == "score":
                        _, t, h, kc = item
                        if kc == 0 and h == 0 and t == 0:
                            pe.wait_ge(side_read, number)
                        mm = nc.tensor.matmul(dst, QA[0:96, h, t * P:(t + 1) * P],
                                              K[0:96, h, kc * CHUNK:(kc + 1) * CHUNK], start=True, stop=True)
                    if kind == "maximum":
                        pe.wait_ge(spread_ready, QT * c + item[1] + 1)
                        for h in range(HEADS):
                            mm = nc.tensor.transpose(dst[0:98, h * P:(h + 1) * P], spread[:, h, :], ident[:, :])
                    if kind == "xr":
                        mm = nc.tensor.matmul(dst, ws_sb[:, :], xt[:, :], start=True, stop=True)
                    if kind == "logit":
                        pe.wait_ge(att_ready, c + 1)
                        nc.tensor.matmul(dst, wb_rep[:, 0, :], att[:, :], start=True, stop=False)
                        mm = nc.tensor.matmul(dst, wb_rep[:, 1, :], xr[:, :], start=False, stop=True)
                    if kind == "turn":
                        pe.wait_ge(mixed_ready, c + 1)
                        for t in range(QT):
                            mm = nc.tensor.transpose(dst[:, t * P:(t + 1) * P], mixed[:, t * P:(t + 1) * P],
                                                     ident[:, :])
                    mm.then_inc(side_done, 1)

                def sides(items, c, base, j):
                    for item in items:
                        chunk = c - 1 if item[0] in ("logit", "turn") else c + 1
                        side(item, chunk, base + j, side_bank(c, j))
                        j += 1
                    return j

                def score(c, t, h):
                    if t == 0 and h == 0:
                        pe.wait_ge(queries_ready, c + 1)
                    if t % 2 == 0 and h == 0:
                        pe.wait_ge(mask_t_ready, (NT // 2) * c + t // 2 + 1)
                    at_least(pe, exp_done, HEADS * (NT * c + t) + h - 1)
                    nc.tensor.matmul(bank(h % 2), ident_b[:, :], mask_t[:, (t // 2) % 2, t % 2, :],
                                     start=True, stop=False)
                    nc.tensor.matmul(bank(h % 2), K[0:98, h, t * P:(t + 1) * P], QB[0:98, h, :],
                                     start=False, stop=True).then_inc(scores_done, 1)

                def sum_values(c, t):
                    pe.wait_ge(exp_done, HEADS * (NT * c + t + 1))
                    if t == 0:
                        at_least(pe, sums_read, c)
                    for h in range(HEADS):
                        mm = nc.tensor.matmul(bank(OUT_BANK)[h * C:(h + 1) * C, :], values[:, t, h * C:(h + 1) * C],
                                              E[:, exp_slot(t), h * CHUNK:(h + 1) * CHUNK],
                                              start=(t == 0), stop=(t == NT - 1))
                    mm.then_inc(summed, 1)

                def count_pair(c, q):
                    pe.wait_ge(pair_added, 2 * (PAIRS * c + q + 1))
                    if q == 0:
                        at_least(pe, denoms_read, c)
                    for h in range(HEADS):
                        mm = nc.tensor.matmul(bank(DEN_BANK)[h * C:(h + 1) * C, :], ones[:, :],
                                              E[:, q % 2, h * CHUNK:(h + 1) * CHUNK],
                                              start=(q == 0), stop=(q == PAIRS - 1))
                    mm.then_inc(counted, 1)

                def body(c, with_prep, with_finish):
                    order = side_order(with_prep, with_finish)
                    j, base = 0, side_base(c)
                    for t in range(NT):
                        items = order[t]
                        if t == 0:
                            j = sides(items[0:1], c, base, j)
                            if with_finish:
                                sum_values(c - 1, NT - 1)
                            for h in range(HEADS):
                                j = sides(items[1 + h:2 + h], c, base, j)
                                score(c, t, h)
                            continue
                        score(c, t, 0)
                        score(c, t, 1)
                        j = sides(items[0:2], c, base, j)
                        score(c, t, 2)
                        j = sides(items[2:3], c, base, j)
                        score(c, t, 3)
                        sum_values(c, t - 1)
                        j = sides(items[3:5], c, base, j)
                        if t % 2 == 1 and t > 1:
                            count_pair(c, (t - 3) // 2)
                        elif t == 1 and with_finish:
                            count_pair(c - 1, PAIRS - 1)
                        j = sides(items[5:], c, base, j)

                pe.wait_ge(keys_split, HEADS * NC)
                pe.wait_ge(values_ready, NC)
                prep = [item for items in side_order(True, False) for item in items]
                sides(prep, -1, 0, 0)
                pe.wait_ge(setup_pool, 8)
                body(0, True, False)
                with pe.Fori(1, NC - 1) as c:
                    body(c, True, True)
                body(NC - 1, False, True)
                sum_values(NC - 1, NT - 1)
                count_pair(NC - 1, PAIRS - 1)
                base = side_base(NC - 1) + FINISH
                finish = [item for items in side_order(False, True) for item in items]
                sides(finish, NC, base, 0)

            @block.vector
            def _(dve):
                chain = Chain(dve, part2_chain)
                scale = float(C) ** -0.5
                nc.vector.tensor_scalar(wq_sb[:, :, :], wq_sb[:, :, :], scale, None, ALU.mult).then_inc(head_setup, 1)
                nc.vector.tensor_scalar(bq_sb[:, :], bq_sb[:, :], scale, None, ALU.mult).then_inc(head_setup, 1)
                nc.vector.tensor_tensor(wb_rep[:, 0, :], wb_sb[:, 0:1].broadcast_to([P, P]),
                                        wb_sb[:, 2:3].broadcast_to([P, P]), ALU.add).then_inc(head_setup, 1)
                nc.vector.tensor_tensor(wb_rep[:, 1, :], wb_sb[:, 1:2].broadcast_to([P, P]),
                                        wb_sb[:, 2:3].broadcast_to([P, P]), ALU.subtract).then_inc(head_setup, 1)
                dve.wait_ge(head_setup, 4)

                def keys(c):
                    where, tiles_ = slice(c * CHUNK, (c + 1) * CHUNK), slice(QT * c, QT * (c + 1))
                    for h in range(HEADS):
                        dve.wait_ge(keys_hi, HEADS * c + h + 1)
                        nc.vector.scalar_tensor_tensor(
                            K[32:64, h, where], bank(1 + h)[32:64, :], bk_sb[32:64, h:h + 1],
                            K[32:64, h, where].bitcast(F32), op0=ALU.add, op1=ALU.subtract).then_inc(keys_split, 1)
                    dve.wait_ge(values_done, c + 1)
                    nc.vector.tensor_tensor(values[:, tiles_, :], bank(5).rearrange("p (t d) -> p t d", d=D),
                                            rows[:, RBV:RBV + 1, :].broadcast_to([P, QT, D]), ALU.add)\
                        .then_inc(values_ready, 1)

                def make_mask_t(c, j):
                    dve.wait_ge(raw_t_in[j % 2], 16 * ((NT // 4) * c + j // 2 + 1))
                    at_least(dve, scores_done, HEADS * (NT * c + 2 * (j - 1)))
                    nc.vector.tensor_scalar(mask_t[:, j % 2, :, :], raw_t[:, j % 2, :, :], 0.0, -BIG,
                                            ALU.is_equal, ALU.mult).then_inc(mask_t_ready, 1)

                def make_mask_q(c, t, quarter):
                    dve.wait_ge(raw_q_in[quarter % 2], 16 * (2 * (QT * c + t) + quarter // 2 + 1))
                    nc.vector.tensor_scalar(mask_q[:, t % 2, quarter * 2 * CHUNK:(quarter + 1) * 2 * CHUNK],
                                            raw_q[:, quarter % 2, :], 0.0, -BIG, ALU.is_equal, ALU.mult)\
                        .then_inc(mask_q_ready, 1)

                def side(item, c, base, j, src):
                    number, kind = base + j, item[0]
                    dve.wait_ge(side_done, number + 1)
                    if kind == "x":
                        nc.vector.tensor_copy(xt[:, :], src).then_inc(side_read, 1)
                    if kind == "query":
                        h = item[1]
                        dve.wait_ge(query_hi, HEADS * c + h + 1)
                        nc.vector.scalar_tensor_tensor(
                            QA[64:96, h, :], src[64:96, :], bq_sb[64:96, h:h + 1], QA[64:96, h, :].bitcast(F32),
                            op0=ALU.add, op1=ALU.subtract).then_inc(side_read, 1)
                    if kind == "score":
                        _, t, h, kc = item
                        if kc % 2 == 0:
                            dve.wait_ge(mask_q_ready, 4 * (QT * c + t) + kc // 2 + 1)
                        at_least(dve, side_read, number - 3)
                        nc.vector.tensor_tensor_reduce(
                            out=masked[:, j % 4, :], in0=src,
                            in1=mask_q[:, t % 2, kc * CHUNK:(kc + 1) * CHUNK], scale=1.0, scalar=-3e38,
                            op0=ALU.add, op1=ALU.max, accum_out=maxima[:, h, kc:kc + 1]).then_inc(side_read, 1)
                        if kc == KC - 1 and QT * c + t + 1 < NT:
                            make_mask_q(*divmod(QT * c + t + 1, QT), h)
                        if kc == KC - 1 and h == HEADS - 1:
                            row_maxima(number)
                    if kind == "maximum":
                        t = item[1]
                        nc.vector.tensor_copy(QA[96:98, :, t * P:(t + 1) * P],
                                              src[96:98, :].rearrange("p (h n) -> p h n", h=HEADS))\
                            .then_inc(side_read, 1)
                    if kind == "xr":
                        nc.vector.tensor_scalar(xr_next[:, :], src, cols[:, BS:BS + 1], None, ALU.add)\
                            .then_inc(side_read, 1)
                    if kind == "logit":
                        nc.vector.tensor_copy(beta[:, :], src).then_inc(side_read, 1)
                    if kind == "turn":
                        at_least(dve, y_out, 16 * c)
                        for t in range(QT):
                            add = nc.vector.tensor_tensor(
                                y[:, t, :].rearrange("p (c h) -> p c h", h=HEADS),
                                src[:, t * P:(t + 1) * P].rearrange("p (h c) -> p c h", h=HEADS),
                                V[:, QT * c + t, :].rearrange("p (c h) -> p c h", h=HEADS), ALU.add)
                        add.then_inc(side_read, 1)
                        dve.wait_ge(side_read, number + 1)
                        norm_begin(chain, QT, y)

                def row_maxima(number):
                    dve.wait_ge(side_read, number + 1)
                    chain.link(nc.vector.tensor_reduce(row_max[:, :], maxima[:, :, :], AX.X, ALU.max))
                    chain.link(nc.vector.scalar_tensor_tensor(row_max[:, :], row_max[:, :], -BIG / 10, row_max[:, :],
                                                              op0=ALU.is_gt, op1=ALU.mult))
                    chain.link(nc.vector.tensor_scalar(minus_hi[:, :], row_max[:, :], -1.0, None, ALU.mult))
                    chain.link(nc.vector.tensor_copy(spread[:, :, 96], minus_hi[:, :].bitcast(F32)))
                    nc.vector.scalar_tensor_tensor(spread[:, :, 97], row_max[:, :], -1.0, minus_hi[:, :].bitcast(F32),
                                                   op0=ALU.mult, op1=ALU.subtract).then_inc(spread_ready, 1)

                def sides(items, c, base, j):
                    for item in items:
                        side(item, c - 1 if item[0] in ("logit", "turn") else c + 1, base, j, side_bank(c, j))
                        j += 1
                    return j

                def divide(c, tile):
                    part_ = slice(tile * P, (tile + 1) * P)
                    if tile == 0:
                        dve.wait_ge(denoms_read, c + 1)
                        chain.link(nc.vector.scalar_tensor_tensor(denom[:, :], denom[:, :], 0.0, denom[:, :],
                                                                  op0=ALU.is_equal, op1=ALU.add))
                    chain.link(nc.vector.reciprocal(denom[:, part_], denom[:, part_]))
                    if tile == QT - 1:
                        dve.wait_ge(sums_read, c + 1)
                        nc.vector.tensor_tensor(att[:, :], att[:, :], denom[:, :], ALU.mult).then_inc(att_ready, 1)

                def mix(c):
                    chain.link(nc.vector.tensor_tensor(xr[:, :], xr[:, :], att[:, :], ALU.subtract))
                    dve.wait_ge(gate_ready, c + 1)
                    chain.link(nc.vector.tensor_tensor(xr[:, :], xr[:, :], beta[:, :], ALU.mult))
                    nc.vector.tensor_tensor(mixed[:, :], xr[:, :], att[:, :], ALU.add).then_inc(mixed_ready, 1)

                def finish_norm(c):
                    norm_end(dve, 12 + c, QT, y, y).then_inc(y_ready, 1)

                def body(c, with_prep, with_finish):
                    order = side_order(with_prep, with_finish)
                    j, base = 0, side_base(c)
                    for t in range(NT):
                        if t % 2 == 0 and t + 2 < NT:
                            make_mask_t(c, t // 2 + 1)
                        elif t % 2 == 0 and with_prep:
                            make_mask_t(c + 1, 0)
                        if with_finish and DIVIDE_AT <= t < DIVIDE_AT + QT:
                            divide(c - 1, t - DIVIDE_AT)
                        if with_finish and t == MIX_AT:
                            mix(c - 1)
                        if t == MIX_AT:
                            if with_finish:
                                dve.wait_ge(mixed_ready, c)
                            chain.link(nc.vector.tensor_copy(xr[:, :], xr_next[:, :]))
                        if with_finish and t == NORM_AT:
                            finish_norm(c - 1)
                        j = sides(order[t], c, base, j)

                for c in range(NC):
                    keys(c)
                for quarter in range(4):
                    make_mask_q(0, 0, quarter)
                prep = [item for items in side_order(True, False) for item in items]
                dve.wait_ge(setup_pool, 7)
                sides(prep, -1, 0, 0)
                make_mask_t(0, 0)
                for c in range(NC):
                    body(c, c < NC - 1, c > 0)
                base = side_base(NC - 1) + FINISH
                for tile in range(QT):
                    divide(NC - 1, tile)
                sides([("logit",)], NC, base, 0)
                mix(NC - 1)
                sides([("turn",)], NC, base, 1)
                finish_norm(NC - 1)


def kernel(**inputs):
    import numpy as np
    import concourse.bacc as bacc
    from concourse import mybir as _mybir
    from concourse.bass_utils import run_bass_kernel_spmd

    a = {name: np.asarray(value) for name, value in inputs.items()}
    w_ih, w_hh = (a["L1_gnn_" + n].reshape(3, D, D) for n in ("W_ih", "W_hh"))
    b_ih, b_hh = (a["L1_gnn_" + n].reshape(3, D) for n in ("b_ih", "b_hh"))
    mats = [a["L0_gnn_" + n] for n in ("uv_W1", "uv_W2", "uv_W3", "vu_W1", "vu_W2", "vu_W3")]
    mats += [a["L1_gnn_W_msg"].T] + [w_ih[g].T for g in range(3)] + [w_hh[g].T for g in range(3)]
    mats += [a["L2_gnn_W_in"], a["L2_gnn_W_out"]]

    def by_head(columns):
        return np.swapaxes(columns.reshape(columns.shape[:-1] + (C, HEADS)), -1, -2).reshape(columns.shape)

    def thrice(w):
        return np.tile(w.reshape(D, HEADS, 1, C), (1, 1, 3, 1)).reshape(D, HEADS, 3 * C)

    cols = [a["L0_gnn_" + n] for n in ("uv_b1", "uv_b2", "vu_b1", "vu_b2")] + [a["L1_gnn_b_msg"]]
    cols += list(b_ih) + list(b_hh) + [by_head(a["L3_gnn_bs"])]
    arrays = {
        "x": a["x"],
        "adj": a["adj"],
        "adj_t": a["adj"].T,
        "weights": np.stack(mats, axis=1),
        "bias_cols": np.stack(cols, axis=1),
        "bias_rows": np.stack([a["L0_gnn_uv_b3"], a["L0_gnn_vu_b3"], a["L3_gnn_bv"]]),
        "wq_rep": thrice(a["L3_gnn_Wq"]),
        "wk_rep": thrice(a["L3_gnn_Wk"]),
        "bq_rep": np.tile(a["L3_gnn_bq"].reshape(HEADS, C).T, (3, 1)),
        "bk_rep": np.tile(a["L3_gnn_bk"].reshape(HEADS, C).T, (3, 1)),
        "wv": a["L3_gnn_Wv"],
        "ws_perm": by_head(a["L3_gnn_Ws"]),
        "wb_cols": by_head(a["L3_gnn_Wb"].reshape(3, D)).T,
    }
    nc = bacc.Bacc("TRN2", target_bir_lowering=False, num_devices=1)
    fed, args = {}, []
    for name, value in arrays.items():
        value = np.ascontiguousarray(value)
        fed[f"{name}_dram"] = value
        args.append(nc.dram_tensor(f"{name}_dram", value.shape, _mybir.dt.from_np(value.dtype),
                                   kind="ExternalInput").ap())
    out = nc.dram_tensor("out_dram", (N, D), _mybir.dt.float32, kind="ExternalOutput").ap()
    graph_kernel(nc, *args, out)
    result = run_bass_kernel_spmd(nc, [fed], core_ids=[0])
    return result.results[0]["out_dram"]
```
